# Optimizing a Trainium2 kernel written in Bass

```python
import numpy as np
import jax
import jax.numpy as jnp

def _softmax(x, axis=-1):
    return jax.nn.softmax(x, axis=axis)

def _gelu(x):
    return jax.nn.gelu(x, approximate=True)

def _silu(x):
    return jax.nn.silu(x)

def _sigmoid(x):
    return jax.nn.sigmoid(x)

def _layernorm(x, axis=-1, eps=1e-05):
    m = jnp.mean(x, axis=axis, keepdims=True)
    v = jnp.var(x, axis=axis, keepdims=True)
    return (x - m) / jnp.sqrt(v + eps)

def _scatter_add(tgt, idx, src, axis=0):
    return tgt.at[idx].add(src)

def _segment_sum(src, seg, n):
    return jax.ops.segment_sum(src, seg, n)
kernel_name = 'mk_adj_resnorm_d4_adj_r2_6d04e7'

def setup_inputs(seed: int=0):
    np.random.seed(seed)
    _w = jnp.asarray

    def _rec_inputs():
        import jax
        import jax.numpy as jnp
        _gk = jax.random.key(seed)
        x = -0.0003929 + 0.9999 * jax.random.normal(jax.random.fold_in(_gk, 1), (64, 128, 256), jnp.float32)
        _a = jax.random.bernoulli(jax.random.fold_in(_gk, 2), 0.03125, (64, 128, 128))
        _a = jnp.logical_or(_a, jnp.eye(128, dtype=bool))
        _af = _a.astype(jnp.float32)
        _af = _af * jax.random.uniform(jax.random.fold_in(_gk, 3), (64, 128, 128), jnp.float32, 0.05, 1)
        adj = _af
        return (x, adj)
    x, adj = _rec_inputs()

    def _L0_gnn_setup():
        import jax, jax.numpy as jnp
        import numpy as np
        EPS = 1e-06
        key = jax.random.key(seed)
        k1, k2, k3 = jax.random.split(key, 3)
        B, N, F, O = (8, 2048, 256, 256)
        x = jax.random.normal(k1, (B, N, F), dtype=jnp.float32)
        adj = jax.random.uniform(k2, (B, N, N), dtype=jnp.float32)
        W = jax.random.normal(k3, (O, 2 * F), dtype=jnp.float32) * (1.0 / np.sqrt(2 * F))
        return {'x': x, 'adj': adj, 'W': W}
    _L0_gnn_all = _L0_gnn_setup()
    _L0_gnn_in = {k: v for k, v in _L0_gnn_all.items() if k in ('W',)}
    del _L0_gnn_all

    def _L1_gnn_setup():
        import jax, jax.numpy as jnp
        import numpy as np
        EPS_LN = 1e-05

        def hypergraph_conv(x, adj, W, b):
            N, C, _ = adj.shape
            H = (adj != 0).astype(x.dtype)
            w = adj.reshape(N, -1)[:, :C]
            xw = jnp.einsum('ncd,hd->nch', x, W)
            Dn = jnp.einsum('nce,ne->nc', H, w)
            Dn = jnp.where(Dn > 0, 1.0 / Dn, 0.0)
            Be = H.sum(axis=1)
            Be = jnp.where(Be > 0, 1.0 / Be, 0.0)
            m = Be[:, :, None] * jnp.einsum('nce,nch->neh', H, xw)
            out = Dn[:, :, None] * jnp.einsum('nce,neh->nch', H, m)
            return out + b

        def layer_norm(x, g, b):
            mu = jnp.mean(x, axis=-1, keepdims=True)
            var = jnp.var(x, axis=-1, keepdims=True)
            return (x - mu) * jax.lax.rsqrt(var + EPS_LN) * g + b
        key = jax.random.key(seed)
        ks = jax.random.split(key, 4)
        N, C, Din, Dh, Dout = (16, 512, 256, 512, 256)
        x = jax.random.normal(ks[0], (N, C, Din), dtype=jnp.float32)
        adj = jax.random.uniform(ks[1], (N, C, C), dtype=jnp.float32, minval=0.1, maxval=1.0)
        W1 = jax.random.normal(ks[2], (Dh, Din), dtype=jnp.float32) * (1.0 / np.sqrt(Din))
        b1 = jnp.zeros((Dh,), dtype=jnp.float32)
        gamma = jnp.ones((Dh,), dtype=jnp.float32)
        beta = jnp.zeros((Dh,), dtype=jnp.float32)
        W2 = jax.random.normal(ks[3], (Dout, Dh), dtype=jnp.float32) * (1.0 / np.sqrt(Dh))
        b2 = jnp.zeros((Dout,), dtype=jnp.float32)
        return {'x': x, 'adj': adj, 'W1': W1, 'b1': b1, 'gamma': gamma, 'beta': beta, 'W2': W2, 'b2': b2}
    _L1_gnn_all = _L1_gnn_setup()
    _L1_gnn_in = {k: v for k, v in _L1_gnn_all.items() if k in ('W1', 'b1', 'gamma', 'beta', 'W2', 'b2')}
    del _L1_gnn_all

    def _L2_gnn_setup():
        import jax, jax.numpy as jnp
        import numpy as np
        B, N, C_IN, C_OUT = (8, 2048, 256, 256)
        key = jax.random.key(seed)
        k1, k2, k3, k4 = jax.random.split(key, 4)
        node_features = jax.random.normal(k1, (B, N, C_IN), dtype=jnp.float32)
        adj_matrix = jax.random.uniform(k2, (B, N, N), dtype=jnp.float32)
        W = jax.random.normal(k3, (C_IN, C_OUT), dtype=jnp.float32) / np.sqrt(C_IN)
        b = jax.random.normal(k4, (C_OUT,), dtype=jnp.float32) * 0.01
        return {'node_features': node_features, 'adj_matrix': adj_matrix, 'W': W, 'b': b}
    _L2_gnn_all = _L2_gnn_setup()
    _L2_gnn_in = {k: v for k, v in _L2_gnn_all.items() if k in ('W', 'b')}
    del _L2_gnn_all

    def _L3_gnn_setup():
        import jax, jax.numpy as jnp
        import numpy as np
        IN_F = 256
        OUT_F = 256
        ALPHA = 0.2
        NEG_INF = -9000000000000000.0
        key = jax.random.key(seed)
        k1, k2, k3, k4 = jax.random.split(key, 4)
        B, S = (8, 1024)
        hidden_state = jax.random.normal(k1, (B, S, IN_F), dtype=jnp.float32)
        adjacent_matrix = jax.random.uniform(k2, (B, S, S), dtype=jnp.float32)
        bound = 1.0 / np.sqrt(IN_F)
        W = jax.random.uniform(k3, (IN_F, OUT_F), dtype=jnp.float32, minval=-bound, maxval=bound)
        a_bound = 1.414 * np.sqrt(6.0 / (2 * OUT_F + 1))
        a = jax.random.uniform(k4, (2 * OUT_F, 1), dtype=jnp.float32, minval=-a_bound, maxval=a_bound)
        return {'hidden_state': hidden_state, 'adjacent_matrix': adjacent_matrix, 'W': W, 'a': a}
    _L3_gnn_all = _L3_gnn_setup()
    _L3_gnn_in = {k: v for k, v in _L3_gnn_all.items() if k in ('W', 'a')}
    del _L3_gnn_all
    return {'x': x, 'adj': adj, 'L0_gnn_W': _L0_gnn_in['W'], 'L1_gnn_W1': _L1_gnn_in['W1'], 'L1_gnn_b1': _L1_gnn_in['b1'], 'L1_gnn_gamma': _L1_gnn_in['gamma'], 'L1_gnn_beta': _L1_gnn_in['beta'], 'L1_gnn_W2': _L1_gnn_in['W2'], 'L1_gnn_b2': _L1_gnn_in['b2'], 'L2_gnn_W': _L2_gnn_in['W'], 'L2_gnn_b': _L2_gnn_in['b'], 'L3_gnn_W': _L3_gnn_in['W'], 'L3_gnn_a': _L3_gnn_in['a']}

def reference(x, adj, L0_gnn_W, L1_gnn_W1, L1_gnn_b1, L1_gnn_gamma, L1_gnn_beta, L1_gnn_W2, L1_gnn_b2, L2_gnn_W, L2_gnn_b, L3_gnn_W, L3_gnn_a):
    import jax
    import jax.numpy as jnp

    def _L0_gnn_ref(x, adj, W):
        import jax, jax.numpy as jnp
        import numpy as np
        EPS = 1e-06
        deg = jnp.sum(adj, axis=-1, keepdims=True)
        agg = jnp.einsum('bij,bjf->bif', adj, x) / jnp.maximum(deg, EPS)
        cat = jnp.concatenate([x, agg], axis=2)
        out = jnp.einsum('bnf,of->bno', cat, W)
        return jax.nn.relu(out)

    def _L1_gnn_ref(x, adj, W1, b1, gamma, beta, W2, b2):
        import jax, jax.numpy as jnp
        import numpy as np
        EPS_LN = 1e-05

        def hypergraph_conv(x, adj, W, b):
            N, C, _ = adj.shape
            H = (adj != 0).astype(x.dtype)
            w = adj.reshape(N, -1)[:, :C]
            xw = jnp.einsum('ncd,hd->nch', x, W)
            Dn = jnp.einsum('nce,ne->nc', H, w)
            Dn = jnp.where(Dn > 0, 1.0 / Dn, 0.0)
            Be = H.sum(axis=1)
            Be = jnp.where(Be > 0, 1.0 / Be, 0.0)
            m = Be[:, :, None] * jnp.einsum('nce,nch->neh', H, xw)
            out = Dn[:, :, None] * jnp.einsum('nce,neh->nch', H, m)
            return out + b

        def layer_norm(x, g, b):
            mu = jnp.mean(x, axis=-1, keepdims=True)
            var = jnp.var(x, axis=-1, keepdims=True)
            return (x - mu) * jax.lax.rsqrt(var + EPS_LN) * g + b
        h = jax.nn.relu(hypergraph_conv(x, adj, W1, b1))
        h = layer_norm(h, gamma, beta)
        y = hypergraph_conv(h, adj, W2, b2)
        return y + x

    def _L2_gnn_ref(node_features, adj_matrix, W, b):
        import jax, jax.numpy as jnp
        import numpy as np
        B, N, C_IN, C_OUT = (8, 2048, 256, 256)
        num_neighbours = adj_matrix.sum(axis=-1, keepdims=True)
        h = jnp.einsum('bni,io->bno', node_features, W) + b
        h = jnp.einsum('bnm,bmo->bno', adj_matrix, h)
        return h / num_neighbours

    def _L3_gnn_ref(hidden_state, adjacent_matrix, W, a):
        import jax, jax.numpy as jnp
        import numpy as np
        IN_F = 256
        OUT_F = 256
        ALPHA = 0.2
        NEG_INF = -9000000000000000.0
        Wh = jnp.einsum('bsi,io->bso', hidden_state, W)
        Wh1 = Wh @ a[:OUT_F, :]
        Wh2 = Wh @ a[OUT_F:, :]
        e = Wh1 + jnp.swapaxes(Wh2, 1, 2)
        e = jax.nn.leaky_relu(e, negative_slope=ALPHA)
        attention = jnp.where(adjacent_matrix > 0.5, e, NEG_INF)
        attention = jax.nn.softmax(attention, axis=1)
        h_prime = jnp.einsum('bst,bto->bso', attention, Wh)
        return jax.nn.elu(h_prime)
    x = _layernorm(x + _L0_gnn_ref(x, adj, L0_gnn_W), axis=-1)
    x = _layernorm(x + _L1_gnn_ref(x, adj, L1_gnn_W1, L1_gnn_b1, L1_gnn_gamma, L1_gnn_beta, L1_gnn_W2, L1_gnn_b2), axis=-1)
    x = _layernorm(x + _L2_gnn_ref(x, adj, L2_gnn_W, L2_gnn_b), axis=-1)
    x = _layernorm(x + _L3_gnn_ref(x, adj, L3_gnn_W, L3_gnn_a), axis=-1)
    return x

_drawn_inputs = setup_inputs


def setup_inputs(seed=0):
    import zlib

    import numpy as np

    out = dict(_drawn_inputs(seed))
    spreads = {'L1_gnn_b1': (0.0, 0.1),
     'L1_gnn_gamma': (1.0, 0.2),
     'L1_gnn_beta': (0.0, 0.1),
     'L1_gnn_b2': (0.0, 0.1)}
    factors = {'L2_gnn_b': 7.04}
    for name, (base, spread) in spreads.items():
        noise = np.random.default_rng([zlib.crc32(name.encode()), seed]).standard_normal(out[name].shape)
        drawn = base * np.exp(spread * noise) if base else spread * noise
        out[name] = jnp.asarray(drawn.astype(out[name].dtype))
    for name, factor in factors.items():
        out[name] = (out[name] * factor).astype(out[name].dtype)
    return out
```

```python
from contextlib import ExitStack

import concourse.bass as bass
from concourse import mybir

ALU = mybir.AluOpType
ACT = mybir.ActivationFunctionType
AX = mybir.AxisListType
F32 = mybir.dt.float32
F32R = mybir.dt.float32r

EPS_DEG = 1e-6
EPS_LN = 1e-5
ALPHA = 0.2
NEG_INF = -9000000000000000.0
TINY = 1.1754944e-38
LOWEST = -3.0e38

GROUP = 4
UNROLL = 8
LAG_PREP = 0
LAG_ADJ = 1
LAG_L0 = 3
LAG_L1A = 3
LAG_L1B = 4
LAG_L2 = 5
LAG_L3 = 6


def build(nc, x, x_t, adj, adj_t, edge_w, ident, w0_t, w1_t, b1, gamma, beta, w2_t, b2, w_l2, b_l2,
          w_l3, w_l3_t, attn, out):
    G, P, _, F = x.shape
    GRAPHS = G * GROUP
    KT = F // P
    H = w1_t.shape[2]
    HT = H // P
    DRAIN = LAG_L3

    with ExitStack() as ctx:
        def sb(name, shape, dt=F32):
            return ctx.enter_context(nc.sbuf_tensor(name, shape, dt))

        def bank(name):
            return ctx.enter_context(nc.psum_tensor(name, [P, 512], F32))

        def sem(name):
            return ctx.enter_context(nc.semaphore(name))

        identity = sb("identity", [P, P])
        w0_raw = sb("w0_raw", [P, KT, 2 * F])
        w0_hi = sb("w0_hi", [P, KT, 2 * F], F32R)
        w0_lo = sb("w0_lo", [P, KT, 2 * F], F32R)
        w1_raw = sb("w1_raw", [P, KT, H])
        w1_hi = sb("w1_hi", [P, KT, H], F32R)
        w1_lo = sb("w1_lo", [P, KT, H], F32R)
        w2_raw = sb("w2_raw", [P, HT, F])
        w2_gamma = sb("w2_gamma", [P, HT, F])
        wl2 = sb("wl2", [P, KT, F])
        wl3 = sb("wl3", [P, KT, F])
        wl3_t = sb("wl3_t", [P, KT, F])
        b1_row = sb("b1_row", [P, H])
        b2_row = sb("b2_row", [P, F])
        bl2_row = sb("bl2_row", [P, F])
        gamma_col = sb("gamma_col", [P, HT])
        beta_col = sb("beta_col", [P, HT])
        attn_col = sb("attn_col", [P, 2 * KT])
        w2_beta_row = sb("w2_beta_row", [P, F])
        wa_row = sb("wa_row", [P, 2, F])
        eps_col = sb("eps_col", [P, 1])
        minus_half = sb("minus_half", [P, 1])
        edge_w_sb = sb("edge_w_sb", [P, GRAPHS])

        x_in = sb("x_in", [P, 2, GROUP, F])
        xt_in = sb("xt_in", [P, 2, GROUP, KT, P])
        a_in = sb("a_in", [P, 2, GROUP, P])
        at_in = sb("at_in", [P, 2, GROUP, P])
        out_st = sb("out_st", [P, 2, GROUP, F])

        deg = sb("deg", [P, 2, GROUP])
        deg_max = sb("deg_max", [P, 2, GROUP])
        deg_inv = sb("deg_inv", [P, 2, GROUP])
        deg_raw_inv = sb("deg_raw_inv", [P, 2, GROUP])
        deg_ratio = sb("deg_ratio", [P, 2, GROUP])
        a_norm = sb("a_norm", [P, 2, GROUP, P])
        h_t = sb("h_t", [P, 2, GROUP, P])
        edge_n = sb("edge_n", [P, 2, GROUP])
        edge_n1 = sb("edge_n1", [P, 2, GROUP])
        edge_inv = sb("edge_inv", [P, 2, GROUP])
        s_rhs = sb("s_rhs", [P, 2, GROUP, P + 2])
        mask = sb("mask", [P, 2, GROUP, P])
        penalty = sb("penalty", [P, 2, GROUP, P])
        adj_sb = sb("adj_sb", [P, 8, 2 * P + 2])
        dn_max = sb("dn_max", [P, 8])
        dn_rec = sb("dn_rec", [P, 8])
        dn = sb("dn", [P, 8])
        dn_rowsum = sb("dn_rowsum", [P, 8])

        xt_hi = sb("xt_hi", [P, 2, KT, P], F32R)
        xt_lo = sb("xt_lo", [P, 2, KT, P], F32R)
        pb_sb = sb("pb_sb", [P, 2, F])
        y0 = sb("y0", [P, 2, F])
        x1 = sb("x1", [P, 2, F])
        z_hi = sb("z_hi", [P, 2, KT * P], F32R)
        z_lo = sb("z_lo", [P, 2, KT * P], F32R)
        u = sb("u", [P, 2, H])
        h = sb("h", [P, 2, H])
        hn = sb("hn", [P, 2, H])
        sh_t = sb("sh_t", [P, 2, HT * P])
        base_a = sb("base_a", [P, 2, F])
        base_b = sb("base_b", [P, 2, F])
        base_c = sb("base_c", [P, 2, F])
        base = sb("base", [P, 2, F])
        y1 = sb("y1", [P, 2, F])
        x2 = sb("x2", [P, 2, F])
        x2_b = sb("x2_b", [P, 2, F])
        ax_t = sb("ax_t", [P, 2, KT * P])
        y2 = sb("y2", [P, 2, F])
        x3 = sb("x3", [P, 2, F])
        x3_m1 = sb("x3_m1", [P, 2, F])
        junk = sb("junk", [P, 2, 2, F])
        wh = sb("wh", [P, 2, 2])
        z_att = sb("z_att", [P, 2, P])
        e_att = sb("e_att", [P, 2, P])
        em_att = sb("em_att", [P, 2, P])
        m_att = sb("m_att", [P, 2])
        nm_att = sb("nm_att", [P, 2])
        p_att = sb("p_att", [P, 2, P])
        sum_att = sb("sum_att", [P, 2])
        inv_att = sb("inv_att", [P, 2])
        att_t = sb("att_t", [P, 2, P])
        ax3_t = sb("ax3_t", [P, 2, KT * P])
        exp_h = sb("exp_h", [P, 2, F])
        elu_x = sb("elu_x", [P, 2, F])
        y3 = sb("y3", [P, 2, F])
        NORMS = ("l0", "l1a", "l1b", "l2", "l3")
        stats = {n: sb(f"stats_{n}", [P, 2, 6]) for n in NORMS}
        mean_var = {n: sb(f"mean_var_{n}", [P, 2, 2]) for n in NORMS}
        var_eps = {n: sb(f"var_eps_{n}", [P, 2]) for n in NORMS}
        rstd = {n: sb(f"rstd_{n}", [P, 2]) for n in NORMS}

        bank_l0 = bank("bank_l0")
        bank_conv1 = bank("bank_conv1")
        bank_sh = bank("bank_sh")
        bank_conv2 = bank("bank_conv2")
        bank_agg = bank("bank_agg")
        bank_l2 = bank("bank_l2")
        bank_l3 = bank("bank_l3")
        bank_adj = bank("bank_adj")

        first_loads = sem("first_loads")
        late_loads = sem("late_loads")
        consts_set = sem("consts_set")
        w_rounded = sem("w_rounded")
        w_split = sem("w_split")
        w2_scaled = sem("w2_scaled")
        rows_made = sem("rows_made")
        rows_kept = sem("rows_kept")
        x_loaded = [sem(f"x_loaded{i}") for i in range(2)]
        xt_loaded = [sem(f"xt_loaded{i}") for i in range(2)]
        a_loaded = [sem(f"a_loaded{i}") for i in range(2)]
        at_loaded = [sem(f"at_loaded{i}") for i in range(2)]
        stored = [sem(f"stored{i}") for i in range(2)]
        deg_sum = sem("deg_sum")
        deg_clamped = sem("deg_clamped")
        deg_inverted = sem("deg_inverted")
        deg_raw_inverted = sem("deg_raw_inverted")
        ratio_ready = sem("ratio_ready")
        a_normed = sem("a_normed")
        h_ready = sem("h_ready")
        edges_counted = sem("edges_counted")
        edges_clamped = sem("edges_clamped")
        edges_inverted = sem("edges_inverted")
        s_rhs_ready = sem("s_rhs_ready")
        w_col_ready = sem("w_col_ready")
        mask_ready = sem("mask_ready")
        penalty_ready = sem("penalty_ready")
        dn_clamped = sem("dn_clamped")
        dn_inverted = sem("dn_inverted")
        dn_ready = sem("dn_ready")
        dn_rowsum_ready = sem("dn_rowsum_ready")
        adj_done = sem("adj_done")
        adj_kept = sem("adj_kept")
        xt_rounded = sem("xt_rounded")
        xt_split = sem("xt_split")
        l0_projected = sem("l0_projected")
        pb_kept = sem("pb_kept")
        l0_done = sem("l0_done")
        sx_done = sem("sx_done")
        z_rounded = sem("z_rounded")
        z_split = sem("z_split")
        conv1_done = sem("conv1_done")
        u_ready = sem("u_ready")
        h_relu = sem("h_relu")
        sh_done = sem("sh_done")
        sh_kept = sem("sh_kept")
        conv2_done = sem("conv2_done")
        base_a_ready = sem("base_a_ready")
        base_b_ready = sem("base_b_ready")
        base_c_ready = sem("base_c_ready")
        base_ready = sem("base_ready")
        x2_b_ready = sem("x2_b_ready")
        ax_done = sem("ax_done")
        ax_kept = sem("ax_kept")
        l2_done = sem("l2_done")
        wh1_ready = sem("wh1_ready")
        wh2_ready = sem("wh2_ready")
        src_done = sem("src_done")
        z_att_ready = sem("z_att_ready")
        e_att_ready = sem("e_att_ready")
        em_att_ready = sem("em_att_ready")
        nm_att_ready = sem("nm_att_ready")
        p_att_ready = sem("p_att_ready")
        inv_att_ready = sem("inv_att_ready")
        att_ready = sem("att_ready")
        ax3_done = sem("ax3_done")
        ax3_kept = sem("ax3_kept")
        l3_done = sem("l3_done")
        exp_ready = sem("exp_ready")
        x3_m1_ready = sem("x3_m1_ready")
        elu_x_ready = sem("elu_x_ready")
        y_ready = {n: sem(f"y_{n}_ready") for n in NORMS if n != "l1a"}
        stats_ready = {n: sem(f"stats_{n}_ready") for n in NORMS}
        moments_ready = {n: sem(f"moments_{n}_ready") for n in NORMS}
        var_eps_ready = {n: sem(f"var_eps_{n}_ready") for n in NORMS}
        rstd_ready = {n: sem(f"rstd_{n}_ready") for n in NORMS}
        normed = {n: sem(f"normed_{n}") for n in NORMS}
        y_ready["l1a"] = h_relu

        FIRST, LATE = 3, 11

        def exists(b, k):
            return not isinstance(b, int) or 0 <= b + k < GRAPHS

        def made(eng, s, b, k):
            eng.wait_ge(s, b + (k + 1))

        def freed(eng, s, b, k, ring=2):
            if isinstance(b, int) and b + k - ring < 0:
                return
            eng.wait_ge(s, b + (k - ring + 1))

        def plain(eng):
            eng.wait_ge(consts_set, 3)

        def group_made(eng, s, b, k):
            eng.wait_ge(s, b + (k - k % GROUP + GROUP))

        def pair_made(eng, s, b, k):
            eng.wait_ge(s, b + (k - k % 2 + 2))

        def loaded(eng, sems, b, k):
            eng.wait_ge(sems[k // GROUP % 2], b * 2 + (k // UNROLL * 16 + 16))

        def run(eng, step):
            for k in range(UNROLL):
                step(0, k)
            with eng.Fori(UNROLL, GRAPHS, UNROLL) as b:
                for k in range(UNROLL):
                    step(b, k)
            for k in range(DRAIN):
                step(GRAPHS, k)

        def stage(f, b, k, lag):
            if exists(b, k - lag):
                f(b, k - lag)

        block = ctx.enter_context(nc.Block())

        @block.sync
        def _(sp):
            def load_adj(q, i):
                if not isinstance(q, int):
                    sp.wait_ge(a_normed, q * UNROLL + (i * GROUP - GROUP))
                    sp.wait_ge(w_col_ready, q * UNROLL + (i * GROUP - GROUP))
                    sp.wait_ge(penalty_ready, q * UNROLL + (i * GROUP - GROUP))
                sp.dma_start(at_in[:, i], adj_t[q * 2 + i]).then_inc(at_loaded[i], 16)
                sp.dma_start(a_in[:, i], adj[q * 2 + i]).then_inc(a_loaded[i], 16)

            def load_x(q, i):
                if not isinstance(q, int):
                    sp.wait_ge(xt_split, q * UNROLL + (i * GROUP - GROUP))
                    sp.wait_ge(y_ready["l0"], q * UNROLL + (i * GROUP - GROUP))
                sp.dma_start(xt_in[:, i], x_t[q * 2 + i]).then_inc(xt_loaded[i], 16)
                sp.dma_start(x_in[:, i], x[q * 2 + i]).then_inc(x_loaded[i], 16)

            def store(q, i):
                sp.wait_ge(normed["l3"], q * UNROLL + (i * GROUP + GROUP))
                sp.dma_start(out[q * 2 + i], out_st[:, i]).then_inc(stored[i], 16)

            load_adj(0, 0)
            sp.dma_start(identity[:], ident).then_inc(first_loads, 16)
            sp.dma_start(edge_w_sb[:], edge_w).then_inc(first_loads, 16)
            sp.dma_start(w0_raw[:], w0_t).then_inc(first_loads, 16)
            load_x(0, 0)
            late = ((w1_raw[:], w1_t), (b1_row[:], b1.partition_broadcast(P)),
                    (gamma_col[:], gamma), (beta_col[:], beta), (attn_col[:], attn),
                    (w2_raw[:], w2_t), (wl3_t[:], w_l3_t),
                    (b2_row[:], b2.partition_broadcast(P)), (wl2[:], w_l2),
                    (bl2_row[:], b_l2.partition_broadcast(P)), (wl3[:], w_l3))
            assert len(late) == LATE
            for dst, src in late:
                sp.dma_start(dst, src).then_inc(late_loads, 16)
            load_adj(0, 1)
            load_x(0, 1)
            with sp.Fori(1, GRAPHS // UNROLL) as q:
                for i in range(2):
                    load_adj(q, i)
                    load_x(q, i)
                    store(q - 1, i)
            for i in range(2):
                store(GRAPHS // UNROLL - 1, i)
            for i in range(2):
                sp.wait_ge(stored[i], 16 * (G // 2) + 16)

        @block.tensor
        def _(pe):
            def chunk(t, c):
                return t[:, c * P:(c + 1) * P]

            pe.wait_ge(late_loads, 16 * LATE)
            for c in range(HT):
                mm = pe.matmul(bank_conv2[:, 0:F], beta_col[:, c:c + 1].to_broadcast([P, P]),
                               w2_raw[:, c], start=(c == 0), stop=(c == HT - 1))
            for a in range(2):
                for c in range(KT):
                    col = attn_col[:, a * KT + c:a * KT + c + 1]
                    mm = pe.matmul((bank_l2, bank_l3)[a][:, 0:F], col.to_broadcast([P, P]),
                                   wl3_t[:, c], start=(c == 0), stop=(c == KT - 1))
            mm.then_inc(rows_made, 1)

            def adjacency(b, k):
                s, i, j = k % 8, k // GROUP % 2, k % GROUP
                group_made(pe, a_normed, b, k)
                group_made(pe, s_rhs_ready, b, k)
                group_made(pe, w_col_ready, b, k)
                freed(pe, adj_kept, b, k, 1)
                j_lag = LAG_L3 - LAG_ADJ
                if not isinstance(b, int) or b + k - j_lag >= 0:
                    pe.wait_ge(z_att_ready, b + (k - j_lag + 1))
                pe.transpose(bank_adj[:, 0:P], a_norm[:, i, j], identity[:])
                pe.matmul(bank_adj[:, P:2 * P + 2], h_t[:, i, j], s_rhs[:, i, j],
                          start=True, stop=True).then_inc(adj_done, 1)

            def split_product(psum, hi, lo, w_hi, w_lo, ready):
                for c in range(KT):
                    pe.matmul(psum[:], hi[c], w_hi[:, c], start=(c == 0), stop=False)
                    pe.matmul(psum[:], hi[c], w_lo[:, c], start=False, stop=False)
                    mm = pe.matmul(psum[:], lo[c], w_hi[:, c], start=False, stop=(c == KT - 1))
                mm.then_inc(ready, 1)

            def l0_project(b, k):
                r = k % 2
                made(pe, xt_rounded, b, k)
                made(pe, xt_split, b, k)
                freed(pe, y_ready["l0"], b, k, 1)
                split_product(bank_l0, [xt_hi[:, r, c] for c in range(KT)],
                              [xt_lo[:, r, c] for c in range(KT)], w0_hi, w0_lo, l0_projected)

            def l0_aggregate(b, k):
                made(pe, pb_kept, b, k)
                made(pe, adj_kept, b, k)
                pe.matmul(bank_l0[:, 0:F], adj_sb[:, k % 8, 0:P], pb_sb[:, k % 2],
                          start=False, stop=True, skip_group_check=True).then_inc(l0_done, 1)

            def aggregate(psum, stationary, moving, n, ready):
                for c in range(n):
                    mm = pe.matmul(chunk(psum, c), chunk(stationary, c), moving,
                                   start=True, stop=True)
                mm.then_inc(ready, 1)

            def product(psum, stationary, w, n, ready):
                for c in range(n):
                    mm = pe.matmul(psum[:, 0:F], chunk(stationary, c), w[:, c],
                                   start=(c == 0), stop=(c == n - 1))
                mm.then_inc(ready, 1)

            def conv1_aggregate(b, k):
                made(pe, normed["l0"], b, k)
                freed(pe, z_split, b, k, 1)
                freed(pe, ax_kept, b, k, LAG_L2 - LAG_L1A)
                aggregate(bank_agg, x1[:, k % 2], adj_sb[:, k % 8, P:2 * P], KT, sx_done)

            def conv1_product(b, k):
                r = k % 2
                made(pe, z_split, b, k)
                freed(pe, u_ready, b, k, 1)
                split_product(bank_conv1, [chunk(z_hi[:, r], c) for c in range(KT)],
                              [chunk(z_lo[:, r], c) for c in range(KT)], w1_hi, w1_lo, conv1_done)

            def conv2_aggregate(b, k):
                made(pe, normed["l1a"], b, k)
                freed(pe, sh_kept, b, k, 1)
                aggregate(bank_sh, hn[:, k % 2], adj_sb[:, k % 8, P:2 * P], HT, sh_done)

            def conv2_product(b, k):
                made(pe, sh_kept, b, k)
                freed(pe, y_ready["l1b"], b, k, 1)
                product(bank_conv2, sh_t[:, k % 2], w2_gamma, HT, conv2_done)

            def l2_aggregate(b, k):
                made(pe, normed["l1b"], b, k)
                agg_lag = LAG_L2 - LAG_L1A - 1
                if not isinstance(b, int) or b + k + agg_lag < GRAPHS:
                    made(pe, z_split, b, k + agg_lag)
                aggregate(bank_agg, x2[:, k % 2], adj_sb[:, k % 8, 0:P], KT, ax_done)

            def l2_product(b, k):
                made(pe, ax_kept, b, k)
                freed(pe, ax3_kept, b, k, 2)
                freed(pe, y_ready["l2"], b, k, 1)
                product(bank_l2, ax_t[:, k % 2], wl2, KT, l2_done)

            def l3_sources(b, k):
                made(pe, wh1_ready, b, k)
                adj_ahead = min(LAG_L3 - LAG_ADJ - 1, GRAPHS - 1 - (b + k) if isinstance(b, int) else 8)
                made(pe, adj_kept, b, k + adj_ahead)
                pe.transpose(bank_adj[:, 0:P], wh[:, k % 2, 0:1].to_broadcast([P, P]),
                             identity[:]).then_inc(src_done, 1)

            def l3_aggregate(b, k):
                made(pe, att_ready, b, k)
                younger = min(1, GRAPHS - 1 - (b + k) if isinstance(b, int) else 1)
                made(pe, y_ready["l2"], b, k + younger)
                aggregate(bank_l2, x3[:, k % 2], att_t[:, k % 2], KT, ax3_done)

            def l3_product(b, k):
                made(pe, ax3_kept, b, k)
                freed(pe, elu_ready, b, k, 1)
                product(bank_l3, ax3_t[:, k % 2], wl3, KT, l3_done)

            elu_ready = y_ready["l3"]

            def step(b, k):
                if isinstance(b, int) and b == 0 and k == LAG_L0:
                    pe.wait_ge(w_split, 2)
                    pe.wait_ge(w2_scaled, 1)
                    pe.wait_ge(rows_kept, 1)
                stage(l0_project, b, k, LAG_L0)
                stage(l3_sources, b, k, LAG_L3)
                stage(adjacency, b, k, LAG_ADJ)
                stage(l0_aggregate, b, k, LAG_L0)
                stage(l2_aggregate, b, k, LAG_L2)
                stage(conv2_aggregate, b, k, LAG_L1B)
                stage(l2_product, b, k, LAG_L2)
                stage(conv2_product, b, k, LAG_L1B)
                stage(l3_aggregate, b, k, LAG_L3)
                stage(conv1_aggregate, b, k, LAG_L1A)
                stage(l3_product, b, k, LAG_L3)
                stage(conv1_product, b, k, LAG_L1A)

            run(pe, step)

        @block.scalar
        def _(act):
            act.wait_ge(first_loads, 16 * FIRST)
            act.activation(w0_hi[:], w0_raw[:], ACT.Copy).then_inc(w_rounded, 1)
            act.wait_ge(late_loads, 16 * LATE)
            act.activation(w1_hi[:], w1_raw[:], ACT.Copy).then_inc(w_rounded, 1)

            def edge_weights(b, k):
                i = k // GROUP % 2
                if not isinstance(b, int) or b + k >= 2 * GROUP:
                    act.wait_ge(adj_done, b + (k - GROUP))
                else:
                    act.wait_ge(consts_set, 3)
                loaded(act, at_loaded, b, k)
                act.activation(s_rhs[:, i, :, P:P + 1], at_in[:, i, :, 0:1],
                               ACT.Copy).then_inc(w_col_ready, GROUP)

            def keep_adj(b, k):
                made(act, adj_done, b, k)
                act.activation(adj_sb[:, k % 8], bank_adj[:, 0:2 * P + 2],
                               ACT.Copy).then_inc(adj_kept, 1)

            def round_xt(b, k):
                loaded(act, xt_loaded, b, k)
                freed(act, l0_projected, b, k)
                act.activation(xt_hi[:, k % 2], xt_in[:, k // GROUP % 2, k % GROUP],
                               ACT.Copy).then_inc(xt_rounded, 1)

            def keep_pb(b, k):
                made(act, l0_projected, b, k)
                freed(act, l0_done, b, k)
                act.activation(pb_sb[:, k % 2], bank_l0[:, F:2 * F], ACT.Copy).then_inc(pb_kept, 1)

            def round_z(b, k):
                made(act, sx_done, b, k)
                freed(act, conv1_done, b, k)
                act.activation(z_hi[:, k % 2], bank_agg[:, 0:KT * P], ACT.Copy).then_inc(z_rounded, 1)

            def relu_u(b, k):
                made(act, u_ready, b, k)
                freed(act, normed["l1a"], b, k)
                act.activation(h[:, k % 2], u[:, k % 2], ACT.Relu).then_inc(h_relu, 1)

            def keep_sh(b, k):
                made(act, sh_done, b, k)
                freed(act, conv2_done, b, k)
                act.activation(sh_t[:, k % 2], bank_sh[:], ACT.Copy).then_inc(sh_kept, 1)

            def base_beta(b, k):
                pair_made(act, dn_rowsum_ready, b, k)
                freed(act, base_b_ready, b, k)
                act.activation(base_a[:, k % 2], w2_beta_row[:], ACT.Copy,
                               scale=dn_rowsum[:, k % 8:k % 8 + 1]).then_inc(base_a_ready, 1)

            def keep_ax(b, k):
                made(act, ax_done, b, k)
                freed(act, l2_done, b, k)
                act.activation(ax_t[:, k % 2], bank_agg[:, 0:KT * P], ACT.Copy).then_inc(ax_kept, 1)

            def exp_att(b, k):
                r = k % 2
                made(act, nm_att_ready, b, k)
                freed(act, att_ready, b, k)
                act.activation(p_att[:, r], em_att[:, r], ACT.Exp, bias=nm_att[:, r:r + 1],
                               accum_out=sum_att[:, r:r + 1]).then_inc(p_att_ready, 1)

            def keep_ax3(b, k):
                made(act, ax3_done, b, k)
                freed(act, l3_done, b, k)
                act.activation(ax3_t[:, k % 2], bank_l2[:, 0:KT * P], ACT.Copy).then_inc(ax3_kept, 1)

            def minus_one(b, k):
                made(act, normed["l2"], b, k)
                freed(act, elu_x_ready, b, k)
                act.activation(x3_m1[:, k % 2], x3[:, k % 2], ACT.Copy, bias=-1.0)\
                    .then_inc(x3_m1_ready, 1)

            def exp_elu(b, k):
                made(act, l3_done, b, k)
                freed(act, elu_x_ready, b, k)
                act.activation(exp_h[:, k % 2], bank_l3[:, 0:F], ACT.Exp).then_inc(exp_ready, 1)

            def step(b, k):
                if isinstance(b, int) and b == 0 and k == LAG_L0:
                    act.wait_ge(rows_kept, 1)
                if k % GROUP == 0:
                    stage(edge_weights, b, k, LAG_PREP)
                stage(round_xt, b, k, LAG_L0 - 1)
                stage(keep_pb, b, k, LAG_L0)
                stage(keep_adj, b, k, LAG_ADJ)
                stage(base_beta, b, k, LAG_L1A)
                stage(keep_ax, b, k, LAG_L2)
                stage(keep_sh, b, k, LAG_L1B)
                stage(exp_att, b, k, LAG_L3)
                stage(minus_one, b, k, LAG_L3)
                stage(keep_ax3, b, k, LAG_L3)
                stage(round_z, b, k, LAG_L1A)
                stage(exp_elu, b, k, LAG_L3)
                stage(relu_u, b, k, LAG_L1A)

            run(act, step)

        @block.vector
        def _(dve):
            def norm_moments(n, y, b, k):
                r = k % 2
                freed(dve, moments_ready[n], b, k)
                made(dve, y_ready[n], b, k)
                dve.bn_stats(stats[n][:, r], y[:, r]).then_inc(stats_ready[n], 1)
                plain(dve)
                made(dve, stats_ready[n], b, k)
                freed(dve, normed[n], b, k)
                dve.bn_aggr(mean_var[n][:, r], stats[n][:, r]).then_inc(moments_ready[n], 1)

            def norm_apply(n, y, dst, b, k):
                r = k % 2
                made(dve, rstd_ready[n], b, k)
                dve.tensor_scalar(dst, y[:, r], mean_var[n][:, r, 0:1], rstd[n][:, r:r + 1],
                                  ALU.subtract, ALU.mult).then_inc(normed[n], 1)

            dve.memset(minus_half[:], -0.5).then_inc(consts_set, 1)
            for i in range(2):
                dve.memset(out_st[:, i, 0, 0:1], 0.0).then_inc(stored[i], 16)
            dve.memset(eps_col[:], EPS_LN).then_inc(consts_set, 1)
            dve.memset(s_rhs[:, :, :, P + 1:P + 2], 1.0).then_inc(consts_set, 1)

            def split_w0():
                dve.wait_ge(w_rounded, 1)
                dve.tensor_tensor(w0_lo[:], w0_raw[:], w0_hi[:].bitcast(F32), ALU.subtract)\
                    .then_inc(w_split, 1)

            def late_weights():
                dve.wait_ge(w_rounded, 2)
                dve.tensor_tensor(w1_lo[:], w1_raw[:], w1_hi[:].bitcast(F32), ALU.subtract)\
                    .then_inc(w_split, 1)
                for c in range(HT):
                    ins = dve.tensor_scalar(w2_gamma[:, c], w2_raw[:, c], gamma_col[:, c:c + 1], None,
                                            ALU.mult)
                ins.then_inc(w2_scaled, 1)
                dve.wait_ge(rows_made, 1)
                dve.tensor_copy(w2_beta_row[:], bank_conv2[:, 0:F])
                dve.tensor_copy(wa_row[:, 0], bank_l2[:, 0:F])
                dve.tensor_copy(wa_row[:, 1], bank_l3[:, 0:F]).then_inc(rows_kept, 1)

            def degrees(b, k):
                i = k // GROUP % 2
                loaded(dve, a_loaded, b, k)
                dve.tensor_reduce(deg[:, i], a_in[:, i], AX.X, ALU.add).then_inc(deg_sum, GROUP)
                group_made(dve, deg_sum, b, k)
                dve.tensor_scalar(deg_max[:, i], deg[:, i], EPS_DEG, None, ALU.max)\
                    .then_inc(deg_clamped, GROUP)
                dve.reciprocal(deg_raw_inv[:, i], deg[:, i]).then_inc(deg_raw_inverted, GROUP)
                group_made(dve, deg_clamped, b, k)
                dve.reciprocal(deg_inv[:, i], deg_max[:, i]).then_inc(deg_inverted, GROUP)
                group_made(dve, deg_raw_inverted, b, k)
                dve.tensor_tensor(deg_ratio[:, i], deg_max[:, i], deg_raw_inv[:, i], ALU.mult)\
                    .then_inc(ratio_ready, GROUP)

            def incidence(b, k):
                i = k // GROUP % 2
                loaded(dve, at_loaded, b, k)
                if not isinstance(b, int) or b + k >= 2 * GROUP:
                    dve.wait_ge(adj_done, b + (k - GROUP))
                dve.tensor_scalar(h_t[:, i], at_in[:, i], 0.0, None, ALU.not_equal)\
                    .then_inc(h_ready, GROUP)
                group_made(dve, h_ready, b, k)
                dve.tensor_reduce(edge_n[:, i], h_t[:, i], AX.X, ALU.add)\
                    .then_inc(edges_counted, GROUP)

            def edge_scale(b, k):
                i = k // GROUP % 2
                group_made(dve, edges_counted, b, k)
                dve.tensor_scalar(edge_n1[:, i], edge_n[:, i], 1.0, None, ALU.max)\
                    .then_inc(edges_clamped, GROUP)
                group_made(dve, edges_clamped, b, k)
                dve.reciprocal(edge_inv[:, i], edge_n1[:, i]).then_inc(edges_inverted, GROUP)

            def masks(b, k):
                i = k // GROUP % 2
                dve.tensor_scalar(mask[:, i], at_in[:, i], 0.5, None, ALU.is_gt)\
                    .then_inc(mask_ready, GROUP)
                dve.tensor_scalar(penalty[:, i], at_in[:, i], 0.5, NEG_INF, ALU.is_le, ALU.mult)\
                    .then_inc(penalty_ready, GROUP)

            def node_scale(b, k):
                s = k % 8 - 1
                raw = adj_sb[:, s:s + 2, 2 * P]
                made(dve, adj_kept, b, k)
                dve.tensor_scalar(dn_max[:, s:s + 2], raw, TINY, None, ALU.max).then_inc(dn_clamped, 2)
                pair_made(dve, dn_clamped, b, k)
                dve.reciprocal(dn_rec[:, s:s + 2], dn_max[:, s:s + 2]).then_inc(dn_inverted, 2)
                pair_made(dve, dn_inverted, b, k)
                dve.scalar_tensor_tensor(out=dn[:, s:s + 2], in0=raw, scalar=0.0, in1=dn_rec[:, s:s + 2],
                                         op0=ALU.is_gt, op1=ALU.mult).then_inc(dn_ready, 2)
                pair_made(dve, dn_ready, b, k)
                dve.tensor_tensor(dn_rowsum[:, s:s + 2], dn[:, s:s + 2], adj_sb[:, s:s + 2, 2 * P + 1],
                                  ALU.mult).then_inc(dn_rowsum_ready, 2)

            def l0_residual(b, k):
                r = k % 2
                made(dve, l0_done, b, k)
                loaded(dve, x_loaded, b, k)
                freed(dve, normed["l0"], b, k)
                dve.scalar_tensor_tensor(out=y0[:, r], in0=bank_l0[:, 0:F], scalar=0.0,
                                         in1=x_in[:, k // GROUP % 2, k % GROUP],
                                         op0=ALU.max, op1=ALU.add).then_inc(y_ready["l0"], 1)
                norm_moments("l0", y0, b, k)

            def l0_norm(b, k):
                freed(dve, sx_done, b, k)
                freed(dve, base_c_ready, b, k)
                norm_apply("l0", y0, x1[:, k % 2], b, k)

            def split_z(b, k):
                r = k % 2
                made(dve, z_rounded, b, k)
                freed(dve, conv1_done, b, k)
                dve.tensor_tensor(z_lo[:, r], bank_agg[:, 0:KT * P], z_hi[:, r].bitcast(F32),
                                  ALU.subtract).then_inc(z_split, 1)

            def conv1_bias(b, k):
                r, s = k % 2, k % 8
                made(dve, conv1_done, b, k)
                pair_made(dve, dn_ready, b, k)
                freed(dve, h_relu, b, k)
                dve.scalar_tensor_tensor(out=u[:, r], in0=bank_conv1[:], scalar=dn[:, s:s + 1],
                                         in1=b1_row[:], op0=ALU.mult, op1=ALU.add)\
                    .then_inc(u_ready, 1)

            def hidden_moments(b, k):
                norm_moments("l1a", h, b, k)

            def hidden_norm(b, k):
                freed(dve, sh_done, b, k)
                norm_apply("l1a", h, hn[:, k % 2], b, k)

            def l1_residual(b, k):
                r, s = k % 2, k % 8
                made(dve, conv2_done, b, k)
                made(dve, base_ready, b, k)
                freed(dve, normed["l1b"], b, k)
                dve.scalar_tensor_tensor(out=y1[:, r], in0=bank_conv2[:, 0:F], scalar=dn[:, s:s + 1],
                                         in1=base[:, r], op0=ALU.mult, op1=ALU.add)\
                    .then_inc(y_ready["l1b"], 1)
                norm_moments("l1b", y1, b, k)

            def l1_norm(b, k):
                freed(dve, ax_done, b, k)
                freed(dve, x2_b_ready, b, k)
                norm_apply("l1b", y1, x2[:, k % 2], b, k)

            def l2_residual(b, k):
                r = k % 2
                made(dve, l2_done, b, k)
                made(dve, x2_b_ready, b, k)
                freed(dve, normed["l2"], b, k)
                dve.scalar_tensor_tensor(out=y2[:, r], in0=bank_l2[:, 0:F],
                                         scalar=deg_ratio_ring[:, k % 8:k % 8 + 1],
                                         in1=x2_b[:, r], op0=ALU.mult, op1=ALU.add)\
                    .then_inc(y_ready["l2"], 1)
                norm_moments("l2", y2, b, k)

            deg_ratio_ring = deg_ratio[:].rearrange("p i j -> p (i j)")

            def l2_norm(b, k):
                r = k % 2
                freed(dve, ax3_done, b, k)
                freed(dve, x3_m1_ready, b, k)
                norm_apply("l2", y2, x3[:, r], b, k)
                made(dve, normed["l2"], b, k)
                freed(dve, src_done, b, k)
                dve.tensor_tensor_reduce(junk[:, r, 0], x3[:, r], wa_row[:, 0], 1.0, 0.0,
                                         ALU.mult, ALU.add, wh[:, r, 0:1]).then_inc(wh1_ready, 1)
                dve.tensor_tensor_reduce(junk[:, r, 1], x3[:, r], wa_row[:, 1], 1.0, 0.0,
                                         ALU.mult, ALU.add, wh[:, r, 1:2]).then_inc(wh2_ready, 1)

            def scores(b, k):
                r, i, j = k % 2, k // GROUP % 2, k % GROUP
                made(dve, src_done, b, k)
                made(dve, wh2_ready, b, k)
                group_made(dve, mask_ready, b, k)
                freed(dve, p_att_ready, b, k)
                dve.scalar_tensor_tensor(out=z_att[:, r], in0=bank_adj[:, 0:P], scalar=wh[:, r, 1:2],
                                         in1=mask[:, i, j], op0=ALU.add, op1=ALU.mult)\
                    .then_inc(z_att_ready, 1)
                made(dve, z_att_ready, b, k)
                dve.scalar_tensor_tensor(out=e_att[:, r], in0=z_att[:, r], scalar=ALPHA,
                                         in1=z_att[:, r], op0=ALU.mult, op1=ALU.max)\
                    .then_inc(e_att_ready, 1)
                plain(dve)
                made(dve, e_att_ready, b, k)
                dve.tensor_tensor_reduce(em_att[:, r], e_att[:, r], penalty[:, i, j], 1.0, LOWEST,
                                         ALU.add, ALU.max, m_att[:, r:r + 1]).then_inc(em_att_ready, 1)
                made(dve, em_att_ready, b, k)
                dve.tensor_scalar(nm_att[:, r:r + 1], m_att[:, r:r + 1], -1.0, None, ALU.mult)\
                    .then_inc(nm_att_ready, 1)

            def attention(b, k):
                r = k % 2
                made(dve, p_att_ready, b, k)
                dve.reciprocal(inv_att[:, r:r + 1], sum_att[:, r:r + 1]).then_inc(inv_att_ready, 1)
                made(dve, inv_att_ready, b, k)
                freed(dve, ax3_done, b, k)
                dve.tensor_scalar(att_t[:, r], p_att[:, r], inv_att[:, r:r + 1], None, ALU.mult)\
                    .then_inc(att_ready, 1)

            def elu_residual(b, k):
                r = k % 2
                made(dve, exp_ready, b, k)
                made(dve, x3_m1_ready, b, k)
                dve.scalar_tensor_tensor(out=elu_x[:, r], in0=exp_h[:, r], scalar=1.0,
                                         in1=x3_m1[:, r], op0=ALU.min, op1=ALU.add)\
                    .then_inc(elu_x_ready, 1)
                made(dve, elu_x_ready, b, k)
                freed(dve, normed["l3"], b, k)
                dve.scalar_tensor_tensor(out=y3[:, r], in0=bank_l3[:, 0:F], scalar=0.0,
                                         in1=elu_x[:, r], op0=ALU.max, op1=ALU.add)\
                    .then_inc(y_ready["l3"], 1)
                norm_moments("l3", y3, b, k)

            def l3_norm(b, k):
                i, j = k // GROUP % 2, k % GROUP
                if j == 0:
                    dve.wait_ge(stored[i], b * 2 + (k // UNROLL * 16 + 16))
                norm_apply("l3", y3, out_st[:, i, j], b, k)

            def step(b, k):
                if isinstance(b, int) and b == 0 and k == 1:
                    split_w0()
                if isinstance(b, int) and b == 0 and k == 2:
                    late_weights()
                stage(scores, b, k, LAG_L3)
                stage(l1_norm, b, k, LAG_L2)
                if k % GROUP == 0:
                    stage(degrees, b, k, LAG_PREP)
                    stage(incidence, b, k, LAG_PREP)
                    stage(edge_scale, b, k, LAG_PREP)
                if k % GROUP == 3:
                    stage(masks, b, k - 3, LAG_PREP)
                if (k - LAG_ADJ) % 2 == 1:
                    stage(node_scale, b, k, LAG_ADJ)
                stage(hidden_norm, b, k, LAG_L1B)
                stage(attention, b, k, LAG_L3)
                stage(l0_residual, b, k, LAG_L0)
                stage(l2_residual, b, k, LAG_L2)
                stage(l0_norm, b, k, LAG_L0)
                stage(l1_residual, b, k, LAG_L1B)
                stage(l2_norm, b, k, LAG_L2)
                stage(split_z, b, k, LAG_L1A)
                stage(elu_residual, b, k, LAG_L3)
                stage(conv1_bias, b, k, LAG_L1A)
                stage(hidden_moments, b, k, LAG_L1A)
                stage(l3_norm, b, k, LAG_L3)

            run(dve, step)

        @block.gpsimd
        def _(pool):
            def rsqrt(n, b, k):
                r = k % 2
                made(pool, moments_ready[n], b, k)
                freed(pool, normed[n], b, k)
                pool.tensor_tensor(var_eps[n][:, r:r + 1], mean_var[n][:, r, 1:2], eps_col[:],
                                   ALU.add).then_inc(var_eps_ready[n], 1)
                made(pool, var_eps_ready[n], b, k)
                pool.tensor_tensor(rstd[n][:, r:r + 1], var_eps[n][:, r:r + 1], minus_half[:],
                                   ALU.pow).then_inc(rstd_ready[n], 1)

            def scale_group(b, k):
                i = k // GROUP % 2
                group_made(pool, deg_inverted, b, k)
                if not isinstance(b, int) or b + k >= 2 * GROUP:
                    pool.wait_ge(adj_done, b + (k - GROUP))
                pool.tensor_tensor(a_norm[:, i], a_in[:, i],
                                   deg_inv[:, i].unsqueeze(2).to_broadcast([P, GROUP, P]),
                                   ALU.mult).then_inc(a_normed, GROUP)

            def scale_edges(b, k):
                i = k // GROUP % 2
                group_made(pool, edges_inverted, b, k)
                pool.tensor_tensor(s_rhs[:, i, :, 0:P], h_t[:, i],
                                   edge_inv[:, i].unsqueeze(2).to_broadcast([P, GROUP, P]),
                                   ALU.mult).then_inc(s_rhs_ready, GROUP)

            def split_xt(b, k):
                r = k % 2
                made(pool, xt_rounded, b, k)
                freed(pool, l0_projected, b, k)
                pool.tensor_tensor(xt_lo[:, r], xt_in[:, k // GROUP % 2, k % GROUP],
                                   xt_hi[:, r].bitcast(F32), ALU.subtract).then_inc(xt_split, 1)

            def base_sum(b, k):
                r = k % 2
                made(pool, base_a_ready, b, k)
                made(pool, normed["l0"], b, k)
                freed(pool, base_ready, b, k)
                pool.tensor_tensor(base_b[:, r], base_a[:, r], b2_row[:], ALU.add)\
                    .then_inc(base_b_ready, 1)
                pool.tensor_scalar(base_c[:, r], x1[:, r], 2.0, 0.0, ALU.mult, ALU.add)\
                    .then_inc(base_c_ready, 1)
                made(pool, base_b_ready, b, k)
                made(pool, base_c_ready, b, k)
                freed(pool, y_ready["l1b"], b, k)
                pool.tensor_tensor(base[:, r], base_b[:, r], base_c[:, r], ALU.add)\
                    .then_inc(base_ready, 1)

            def l2_bias(b, k):
                made(pool, normed["l1b"], b, k)
                freed(pool, y_ready["l2"], b, k)
                pool.tensor_tensor(x2_b[:, k % 2], x2[:, k % 2], bl2_row[:], ALU.add)\
                    .then_inc(x2_b_ready, 1)

            def step(b, k):
                if isinstance(b, int) and b == 0 and k == 0:
                    pool.wait_ge(consts_set, 3)
                if isinstance(b, int) and b == 0 and k == LAG_L0:
                    pool.wait_ge(late_loads, 16 * LATE)
                if k % GROUP == 0:
                    stage(scale_group, b, k, LAG_PREP)
                if k % GROUP == 1:
                    stage(scale_edges, b, k - 1, LAG_PREP)
                stage(split_xt, b, k, LAG_L0 - 1)
                stage(l2_bias, b, k, LAG_L2)
                for n, lag in (("l0", LAG_L0),):
                    stage(lambda b, k: rsqrt(n, b, k), b, k, lag)
                stage(lambda b, k: rsqrt("l2", b, k), b, k, LAG_L2)
                stage(base_sum, b, k, LAG_L1A)
                stage(lambda b, k: rsqrt("l1b", b, k), b, k, LAG_L1B)
                stage(lambda b, k: rsqrt("l3", b, k), b, k, LAG_L3)
                stage(lambda b, k: rsqrt("l1a", b, k), b, k, LAG_L1A)

            run(pool, step)


def kernel(x, adj, L0_gnn_W, L1_gnn_W1, L1_gnn_b1, L1_gnn_gamma, L1_gnn_beta, L1_gnn_W2, L1_gnn_b2,
           L2_gnn_W, L2_gnn_b, L3_gnn_W, L3_gnn_a):
    import numpy as np
    import concourse.bacc as bacc
    from concourse.bass_utils import run_bass_kernel_spmd

    x, adj = np.asarray(x), np.asarray(adj)
    n, p, f = x.shape
    groups, kt = n // GROUP, f // p

    def rows(w):
        w = np.asarray(w)
        return w.reshape(w.shape[0] // p, p, w.shape[1]).transpose(1, 0, 2)

    def cols(v):
        return np.asarray(v).reshape(-1, p).T

    w0, w3 = np.asarray(L0_gnn_W), np.asarray(L3_gnn_W)
    arrays = {
        "x_nodes": x.reshape(groups, GROUP, p, f).transpose(0, 2, 1, 3),
        "x_feats": x.reshape(groups, GROUP, p, kt, p).transpose(0, 4, 1, 3, 2),
        "adj_rows": adj.reshape(groups, GROUP, p, p).transpose(0, 2, 1, 3),
        "adj_cols": adj.reshape(groups, GROUP, p, p).transpose(0, 3, 1, 2),
        "edge_w": adj[:, 0, :].T,
        "ident": np.eye(p, dtype=x.dtype),
        "w0_t": rows(np.concatenate([w0[:, :f].T, w0[:, f:].T], axis=1)),
        "w1_t": rows(np.asarray(L1_gnn_W1).T),
        "b1": np.asarray(L1_gnn_b1),
        "gamma": cols(L1_gnn_gamma),
        "beta": cols(L1_gnn_beta),
        "w2_t": rows(np.asarray(L1_gnn_W2).T),
        "b2": np.asarray(L1_gnn_b2),
        "w_l2": rows(L2_gnn_W),
        "b_l2": np.asarray(L2_gnn_b),
        "w_l3": rows(w3),
        "w_l3_t": rows(w3.T),
        "attn": cols(L3_gnn_a),
    }
    nc = bacc.Bacc("TRN2", target_bir_lowering=False, num_devices=1)
    ins, args = {}, []
    for name, a in arrays.items():
        a = np.ascontiguousarray(a)
        ins[f"in_{name}"] = a
        args.append(nc.dram_tensor(f"in_{name}", a.shape, mybir.dt.from_np(a.dtype),
                                   kind="ExternalInput").ap())
    out = nc.dram_tensor("out_x", (groups, p, GROUP, f), F32, kind="ExternalOutput").ap()
    build(nc, *args, out)
    r = run_bass_kernel_spmd(nc, [ins], core_ids=[0])
    got = r.results[0]["out_x"]
    return np.ascontiguousarray(got.transpose(0, 2, 1, 3)).reshape(n, p, f)
```

```python
from contextlib import ExitStack

import concourse.bass as bass
from concourse import mybir

ALU = mybir.AluOpType
ACT = mybir.ActivationFunctionType
AX = mybir.AxisListType
F32 = mybir.dt.float32
F32R = mybir.dt.float32r

EPS_DEG = 1e-6
EPS_LN = 1e-5
ALPHA = 0.2
NEG_INF = -9000000000000000.0
TINY = 1.1754944e-38
LOWEST = -3.0e38

GROUP = 4
UNROLL = 8


def build(nc, x, x_t, adj, adj_t, ident, w0_t, w1_t, b1, gamma, beta, w2_t, b2, w_l2, b_l2,
          w_l3, w_l3_t, attn, out):
    G, P, _, F = x.shape
    GRAPHS = G * GROUP
    KT = F // P
    H = w1_t.shape[2]
    HT = H // P
    DRAIN = 6
    ROOT = F ** -0.5
    assert ROOT * ROOT * F == 1.0

    with ExitStack() as ctx:
        def sb(name, shape, dt=F32):
            return ctx.enter_context(nc.sbuf_tensor(name, shape, dt))

        def bank(name):
            return ctx.enter_context(nc.psum_tensor(name, [P, 512], F32))

        def sem(name):
            return ctx.enter_context(nc.semaphore(name))

        identity = sb("identity", [P, P])
        w0_raw = sb("w0_raw", [P, KT, 2 * F])
        w0_hi = sb("w0_hi", [P, KT, 2 * F], F32R)
        w0_lo = sb("w0_lo", [P, KT, 2 * F], F32R)
        w1_raw = sb("w1_raw", [P, KT, H])
        w1_hi = sb("w1_hi", [P, KT, H], F32R)
        w1_lo = sb("w1_lo", [P, KT, H], F32R)
        w2_raw = sb("w2_raw", [P, HT, F])
        w2_gamma = sb("w2_gamma", [P, HT, F])
        wl2 = sb("wl2", [P, KT, F])
        wl3 = sb("wl3", [P, KT, F])
        wl3_t = sb("wl3_t", [P, KT, F])
        b1_row = sb("b1_row", [P, H])
        b2_row = sb("b2_row", [P, F])
        bl2_row = sb("bl2_row", [P, F])
        gamma_col = sb("gamma_col", [P, HT])
        beta_col = sb("beta_col", [P, HT])
        attn_col = sb("attn_col", [P, 2 * KT])
        w2_beta_row = sb("w2_beta_row", [P, F])
        wa_row = sb("wa_row", [P, 2, F])
        eps_col = sb("eps_col", [P, 1])
        minus_half = sb("minus_half", [P, 1])

        x_in = sb("x_in", [P, 2, GROUP, F])
        xt_in = sb("xt_in", [P, 2, GROUP, KT, P])
        a_in = sb("a_in", [P, 2, GROUP, P])
        at_in = sb("at_in", [P, 2, GROUP, P])
        out_st = sb("out_st", [P, 2, GROUP, F])

        deg = sb("deg", [P, 2, GROUP])
        deg_max = sb("deg_max", [P, 2, GROUP])
        deg_inv = sb("deg_inv", [P, 2, GROUP])
        deg_raw_inv = sb("deg_raw_inv", [P, 2, GROUP])
        deg_ratio = sb("deg_ratio", [P, 2, GROUP])
        a_norm = sb("a_norm", [P, 2, GROUP, P])
        h_t = sb("h_t", [P, 2, GROUP, P])
        edge_n = sb("edge_n", [P, 2, GROUP])
        edge_n1 = sb("edge_n1", [P, 2, GROUP])
        edge_inv = sb("edge_inv", [P, 2, GROUP])
        s_rhs = sb("s_rhs", [P, 2, GROUP, P + 2])
        mask = sb("mask", [P, 2, GROUP, P])
        penalty = sb("penalty", [P, 2, GROUP, P])
        adj_sb = sb("adj_sb", [P, 8, 2 * P + 2])
        dn_max = sb("dn_max", [P, 8])
        dn_rec = sb("dn_rec", [P, 8])
        dn = sb("dn", [P, 8])
        dn_rowsum = sb("dn_rowsum", [P, 8])

        xt_hi = sb("xt_hi", [P, 2, KT, P], F32R)
        xt_lo = sb("xt_lo", [P, 2, KT, P], F32R)
        pb_sb = sb("pb_sb", [P, 2, F])
        y0 = sb("y0", [P, 2, F])
        x1 = sb("x1", [P, 2, F])
        z_hi = sb("z_hi", [P, 2, KT * P], F32R)
        z_lo = sb("z_lo", [P, 2, KT * P], F32R)
        u = sb("u", [P, 2, H])
        h = sb("h", [P, 2, H])
        hn = sb("hn", [P, 2, H])
        sh_t = sb("sh_t", [P, 2, HT * P])
        base_a = sb("base_a", [P, 2, F])
        base_b = sb("base_b", [P, 2, F])
        base_c = sb("base_c", [P, 2, F])
        base = sb("base", [P, 2, F])
        y1 = sb("y1", [P, 2, F])
        x2 = sb("x2", [P, 2, F])
        x2_b = sb("x2_b", [P, 2, F])
        ax_t = sb("ax_t", [P, 2, KT * P])
        y2 = sb("y2", [P, 2, F])
        x3 = sb("x3", [P, 2, F])
        x3_m1 = sb("x3_m1", [P, 2, F])
        junk = sb("junk", [P, 2, 2, F])
        wh = sb("wh", [P, 2, 2])
        z_att = sb("z_att", [P, 2, P])
        e_att = sb("e_att", [P, 2, P])
        em_att = sb("em_att", [P, 2, P])
        m_att = sb("m_att", [P, 2])
        nm_att = sb("nm_att", [P, 2])
        p_att = sb("p_att", [P, 2, P])
        sum_att = sb("sum_att", [P, 2])
        inv_att = sb("inv_att", [P, 2])
        att_t = sb("att_t", [P, 2, P])
        ax3_t = sb("ax3_t", [P, 2, KT * P])
        exp_h = sb("exp_h", [P, 2, F])
        relu_h = sb("relu_h", [P, 2, F])
        elu_x = sb("elu_x", [P, 2, F])
        y3 = sb("y3", [P, 2, F])
        NORMS = ("l0", "l1a", "l1b", "l2", "l3")
        stats = {n: sb(f"stats_{n}", [P, 2, 6]) for n in NORMS}
        mean_var = {n: sb(f"mean_var_{n}", [P, 2, 2]) for n in NORMS}
        var_eps = {n: sb(f"var_eps_{n}", [P, 2]) for n in NORMS}
        ACT_NORMS = ("l0", "l3")
        y_sum = {n: sb(f"y_sum_{n}", [P, 2]) for n in ACT_NORMS}
        shift = {n: sb(f"shift_{n}", [P, 2]) for n in ACT_NORMS}
        squares = {n: sb(f"squares_{n}", [P, 2, F]) for n in ACT_NORMS}
        shift_std = sb("shift_std", [P, 2])
        rstd = {n: sb(f"rstd_{n}", [P, 2]) for n in NORMS}

        bank_l0 = bank("bank_l0")
        bank_conv1 = bank("bank_conv1")
        bank_sh = bank("bank_sh")
        bank_conv2 = bank("bank_conv2")
        bank_agg = bank("bank_agg")
        bank_l2 = bank("bank_l2")
        bank_l3 = bank("bank_l3")
        bank_adj = bank("bank_adj")

        ident_loaded = sem("ident_loaded")
        w0_loaded = sem("w0_loaded")
        x0_loaded = sem("x0_loaded")
        w1_loaded = sem("w1_loaded")
        late_loads = sem("late_loads")
        consts_set = sem("consts_set")
        w0_rounded = sem("w0_rounded")
        w1_rounded = sem("w1_rounded")
        w0_split = sem("w0_split")
        w1_split = sem("w1_split")
        w2_scaled = sem("w2_scaled")
        rows_made = sem("rows_made")
        rows_kept = sem("rows_kept")
        x_loaded = [sem(f"x_loaded{i}") for i in range(2)]
        xt_loaded = [sem(f"xt_loaded{i}") for i in range(2)]
        a_loaded = [sem(f"a_loaded{i}") for i in range(2)]
        at_loaded = [sem(f"at_loaded{i}") for i in range(2)]
        stored = [sem(f"stored{i}") for i in range(2)]
        deg_sum = sem("deg_sum")
        deg_clamped = sem("deg_clamped")
        deg_inverted = sem("deg_inverted")
        deg_raw_inverted = sem("deg_raw_inverted")
        ratio_ready = sem("ratio_ready")
        a_normed = sem("a_normed")
        h_ready = sem("h_ready")
        edges_counted = sem("edges_counted")
        edges_clamped = sem("edges_clamped")
        edges_inverted = sem("edges_inverted")
        s_rhs_ready = sem("s_rhs_ready")
        w_col_ready = sem("w_col_ready")
        mask_ready = sem("mask_ready")
        penalty_ready = sem("penalty_ready")
        dn_clamped = sem("dn_clamped")
        dn_inverted = sem("dn_inverted")
        dn_ready = sem("dn_ready")
        dn_rowsum_ready = sem("dn_rowsum_ready")
        adj_done = sem("adj_done")
        adj_kept = sem("adj_kept")
        xt_rounded = sem("xt_rounded")
        xt_split = sem("xt_split")
        l0_projected = sem("l0_projected")
        pb_kept = sem("pb_kept")
        l0_done = sem("l0_done")
        sx_done = sem("sx_done")
        z_rounded = sem("z_rounded")
        z_split = sem("z_split")
        conv1_done = sem("conv1_done")
        u_ready = sem("u_ready")
        h_relu = sem("h_relu")
        sh_done = sem("sh_done")
        sh_kept = sem("sh_kept")
        conv2_done = sem("conv2_done")
        base_a_ready = sem("base_a_ready")
        base_b_ready = sem("base_b_ready")
        base_c_ready = sem("base_c_ready")
        base_ready = sem("base_ready")
        x2_b_ready = sem("x2_b_ready")
        ax_done = sem("ax_done")
        ax_kept = sem("ax_kept")
        l2_done = sem("l2_done")
        wh1_ready = sem("wh1_ready")
        wh2_ready = sem("wh2_ready")
        src_done = sem("src_done")
        z_att_ready = sem("z_att_ready")
        e_att_ready = sem("e_att_ready")
        em_att_ready = sem("em_att_ready")
        nm_att_ready = sem("nm_att_ready")
        p_att_ready = sem("p_att_ready")
        inv_att_ready = sem("inv_att_ready")
        att_ready = sem("att_ready")
        ax3_done = sem("ax3_done")
        ax3_kept = sem("ax3_kept")
        l3_done = sem("l3_done")
        exp_ready = sem("exp_ready")
        x3_m1_ready = sem("x3_m1_ready")
        relu_h_ready = sem("relu_h_ready")
        elu_x_ready = sem("elu_x_ready")
        y_ready = {n: sem(f"y_{n}_ready") for n in NORMS if n != "l1a"}
        stats_ready = {n: sem(f"stats_{n}_ready") for n in NORMS}
        moments_ready = {n: sem(f"moments_{n}_ready") for n in NORMS}
        var_eps_ready = {n: sem(f"var_eps_{n}_ready") for n in NORMS}
        rstd_ready = {n: sem(f"rstd_{n}_ready") for n in NORMS}
        means_ready = {n: sem(f"means_{n}_ready") for n in ACT_NORMS}
        shift_std_ready = sem("shift_std_ready")
        normed = {n: sem(f"normed_{n}") for n in NORMS}
        y_ready["l1a"] = h_relu
        Y = {"l0": y0, "l1a": h, "l1b": y1, "l2": y2, "l3": y3}

        LATE = 10

        def exists(b, k):
            return not isinstance(b, int) or 0 <= b + k < GRAPHS

        def made(eng, s, b, k):
            eng.wait_ge(s, b + (k + 1))

        def freed(eng, s, b, k, ring=2):
            if isinstance(b, int) and b + k - ring < 0:
                return
            eng.wait_ge(s, b + (k - ring + 1))

        def plain(eng):
            eng.wait_ge(consts_set, 3)

        def group_made(eng, s, b, k):
            eng.wait_ge(s, b + (k - k % GROUP + GROUP))

        def pair_made(eng, s, b, k):
            eng.wait_ge(s, b + (k - k % 2 + 2))

        def loaded(eng, sems, b, k):
            eng.wait_ge(sems[k // GROUP % 2], b * 2 + (k // UNROLL * 16 + 16))

        def run(eng, step):
            for k in range(UNROLL):
                step(0, k)
            with eng.Fori(UNROLL, GRAPHS, UNROLL) as b:
                for k in range(UNROLL):
                    step(b, k)
            for k in range(DRAIN):
                step(GRAPHS, k)

        def first(b, k):
            return isinstance(b, int) and b + k == 0

        def stage(f, b, k, lag, *which):
            if exists(b, k - lag):
                f(b, k - lag, *which)

        def stage_once(f, b, k, lag, *which):
            if first(b, k - lag):
                f(*which)

        def stage_group(f, b, k, lag):
            if (k - lag) % GROUP == 0:
                stage(f, b, k, lag)

        def stage_pair(f, b, k, lag):
            if (k - lag) % 2 == 1:
                stage(f, b, k, lag)

        block = ctx.enter_context(nc.Block())

        @block.sync
        def _(sp):
            def load_adj(q, i):
                if not isinstance(q, int):
                    sp.wait_ge(a_normed, q * UNROLL + (i * GROUP - GROUP))
                    sp.wait_ge(w_col_ready, q * UNROLL + (i * GROUP - GROUP))
                    sp.wait_ge(penalty_ready, q * UNROLL + (i * GROUP - GROUP))
                sp.dma_start(at_in[:, i], adj_t[q * 2 + i]).then_inc(at_loaded[i], 16)
                sp.dma_start(a_in[:, i], adj[q * 2 + i]).then_inc(a_loaded[i], 16)

            def load_x(q, i):
                if not isinstance(q, int):
                    sp.wait_ge(xt_split, q * UNROLL + (i * GROUP - GROUP))
                    sp.wait_ge(y_ready["l0"], q * UNROLL + (i * GROUP - GROUP))
                sp.dma_start(xt_in[:, i], x_t[q * 2 + i]).then_inc(xt_loaded[i], 16)
                sp.dma_start(x_in[:, i], x[q * 2 + i]).then_inc(x_loaded[i], 16)

            def store(q, i):
                sp.wait_ge(normed["l3"], q * UNROLL + (i * GROUP + GROUP))
                sp.dma_start(out[q * 2 + i], out_st[:, i]).then_inc(stored[i], 16)

            sp.dma_start(xt_in[:, 0, 0], x_t[0][:, 0]).then_inc(x0_loaded, 16)
            for c in range(KT):
                sp.dma_start(w0_raw[:, c], w0_t[:, c]).then_inc(w0_loaded, 16)
            load_adj(0, 0)
            sp.dma_start(identity[:], ident).then_inc(ident_loaded, 16)
            sp.dma_start(xt_in[:, 0, 1:GROUP], x_t[0][:, 1:GROUP]).then_inc(xt_loaded[0], 16)
            sp.dma_start(x_in[:, 0], x[0]).then_inc(x_loaded[0], 16)
            sp.dma_start(w1_raw[:], w1_t).then_inc(w1_loaded, 16)
            late = ((b1_row[:], b1.partition_broadcast(P)),
                    (gamma_col[:], gamma), (beta_col[:], beta), (attn_col[:], attn),
                    (w2_raw[:], w2_t), (wl3_t[:], w_l3_t),
                    (b2_row[:], b2.partition_broadcast(P)), (wl2[:], w_l2),
                    (bl2_row[:], b_l2.partition_broadcast(P)), (wl3[:], w_l3))
            assert len(late) == LATE
            for dst, src in late:
                sp.dma_start(dst, src).then_inc(late_loads, 16)
            load_adj(0, 1)
            load_x(0, 1)
            with sp.Fori(1, GRAPHS // UNROLL) as q:
                for i in range(2):
                    load_adj(q, i)
                    load_x(q, i)
                    store(q - 1, i)
            for i in range(2):
                store(GRAPHS // UNROLL - 1, i)
            for i in range(2):
                sp.wait_ge(stored[i], 16 * (G // 2) + 16)

        @block.tensor
        def _(pe):
            def chunk(t, c):
                return t[:, c * P:(c + 1) * P]

            def bank_free(b, k, own, other, ahead):
                if isinstance(b, int):
                    if 0 < b + k:
                        made(pe, own, b, k - 1)
                    if b + k + ahead >= GRAPHS:
                        pe.wait_ge(other, GRAPHS)
                        return
                    if b + k + ahead < 0:
                        return
                made(pe, other, b, k + ahead)

            def constant_rows():
                pe.wait_ge(late_loads, 16 * LATE)
                for c in range(HT):
                    mm = pe.matmul(bank_conv2[:, 0:F], beta_col[:, c:c + 1].to_broadcast([P, P]),
                                   w2_raw[:, c], start=(c == 0), stop=(c == HT - 1))
                for a in range(2):
                    for c in range(KT):
                        col = attn_col[:, a * KT + c:a * KT + c + 1]
                        mm = pe.matmul((bank_l2, bank_l3)[a][:, 0:F], col.to_broadcast([P, P]),
                                       wl3_t[:, c], start=(c == 0), stop=(c == KT - 1))
                mm.then_inc(rows_made, 1)

            def adjacency(b, k):
                s, i, j = k % 8, k // GROUP % 2, k % GROUP
                group_made(pe, a_normed, b, k)
                group_made(pe, s_rhs_ready, b, k)
                group_made(pe, w_col_ready, b, k)
                bank_free(b, k, adj_kept, z_att_ready, -5)
                if first(b, k):
                    pe.wait_ge(ident_loaded, 16)
                pe.transpose(bank_adj[:, 0:P], a_norm[:, i, j], identity[:])
                pe.matmul(bank_adj[:, P:2 * P + 2], h_t[:, i, j], s_rhs[:, i, j],
                          start=True, stop=True).then_inc(adj_done, 1)

            def split_product(psum, hi, lo, w_hi, w_lo, ready):
                for c in range(KT):
                    pe.matmul(psum[:], hi[c], w_hi[:, c], start=(c == 0), stop=False)
                    pe.matmul(psum[:], hi[c], w_lo[:, c], start=False, stop=False)
                    mm = pe.matmul(psum[:], lo[c], w_hi[:, c], start=False, stop=(c == KT - 1))
                mm.then_inc(ready, 1)

            def l0_project(b, k):
                r = k % 2
                made(pe, xt_split, b, k)
                if first(b, k):
                    pe.wait_ge(w0_split, KT)
                freed(pe, y_ready["l0"], b, k, 1)
                split_product(bank_l0, [xt_hi[:, r, c] for c in range(KT)],
                              [xt_lo[:, r, c] for c in range(KT)], w0_hi, w0_lo, l0_projected)

            def l0_aggregate(b, k):
                made(pe, pb_kept, b, k)
                made(pe, adj_kept, b, k)
                pe.matmul(bank_l0[:, 0:F], adj_sb[:, k % 8, 0:P], pb_sb[:, k % 2],
                          start=False, stop=True, skip_group_check=True).then_inc(l0_done, 1)

            def aggregate(psum, stationary, moving, n, ready):
                for c in range(n):
                    mm = pe.matmul(chunk(psum, c), chunk(stationary, c), moving,
                                   start=True, stop=True)
                mm.then_inc(ready, 1)

            def product(psum, stationary, w, n, ready):
                for c in range(n):
                    mm = pe.matmul(psum[:, 0:F], chunk(stationary, c), w[:, c],
                                   start=(c == 0), stop=(c == n - 1))
                mm.then_inc(ready, 1)

            def conv1_aggregate(b, k):
                made(pe, normed["l0"], b, k)
                bank_free(b, k, z_split, ax_kept, -3)
                aggregate(bank_agg, x1[:, k % 2], adj_sb[:, k % 8, P:2 * P], KT, sx_done)

            def conv1_product(b, k):
                r = k % 2
                made(pe, z_split, b, k)
                freed(pe, u_ready, b, k, 1)
                if first(b, k):
                    pe.wait_ge(w1_split, 1)
                split_product(bank_conv1, [chunk(z_hi[:, r], c) for c in range(KT)],
                              [chunk(z_lo[:, r], c) for c in range(KT)], w1_hi, w1_lo, conv1_done)

            def conv2_aggregate(b, k):
                made(pe, normed["l1a"], b, k)
                freed(pe, sh_kept, b, k, 1)
                aggregate(bank_sh, hn[:, k % 2], adj_sb[:, k % 8, P:2 * P], HT, sh_done)

            def conv2_product(b, k):
                made(pe, sh_kept, b, k)
                freed(pe, y_ready["l1b"], b, k, 1)
                if first(b, k):
                    pe.wait_ge(w2_scaled, 1)
                    pe.wait_ge(rows_kept, 1)
                product(bank_conv2, sh_t[:, k % 2], w2_gamma, HT, conv2_done)

            def l2_aggregate(b, k):
                made(pe, normed["l1b"], b, k)
                bank_free(b, k, ax_kept, z_split, 2)
                aggregate(bank_agg, x2[:, k % 2], adj_sb[:, k % 8, 0:P], KT, ax_done)

            def l2_product(b, k):
                made(pe, ax_kept, b, k)
                bank_free(b, k, y_ready["l2"], ax3_kept, -2)
                product(bank_l2, ax_t[:, k % 2], wl2, KT, l2_done)

            def l3_sources(b, k):
                made(pe, wh1_ready, b, k)
                bank_free(b, k, z_att_ready, adj_kept, 4)
                pe.transpose(bank_adj[:, 0:P], wh[:, k % 2, 0:1].to_broadcast([P, P]),
                             identity[:]).then_inc(src_done, 1)

            def l3_aggregate(b, k):
                made(pe, att_ready, b, k)
                bank_free(b, k, ax3_kept, y_ready["l2"], 1)
                aggregate(bank_l2, x3[:, k % 2], att_t[:, k % 2], KT, ax3_done)

            def l3_product(b, k):
                made(pe, ax3_kept, b, k)
                freed(pe, relu_h_ready, b, k, 1)
                product(bank_l3, ax3_t[:, k % 2], wl3, KT, l3_done)

            def step(b, k):
                stage(l0_aggregate, b, k, 2)
                stage(l2_aggregate, b, k, 5)
                stage(conv2_product, b, k, 4)
                stage_once(constant_rows, b, k, 3)
                stage(l2_product, b, k, 5)
                stage(l0_project, b, k, 1)
                stage(l3_aggregate, b, k, 6)
                stage(conv1_aggregate, b, k, 2)
                stage(adjacency, b, k, 1)
                stage(l3_product, b, k, 6)
                stage(conv2_aggregate, b, k, 3)
                stage(conv1_product, b, k, 2)
                stage(l3_sources, b, k, 5)
            run(pe, step)

        @block.scalar
        def _(act):
            def round_w0(c):
                act.wait_ge(w0_loaded, 16 * c + 16)
                act.activation(w0_hi[:, c], w0_raw[:, c], ACT.Copy).then_inc(w0_rounded, 1)

            def round_w1():
                act.wait_ge(w1_loaded, 16)
                act.activation(w1_hi[:], w1_raw[:], ACT.Copy).then_inc(w1_rounded, 1)

            def edge_weights(b, k):
                i = k // GROUP % 2
                if not isinstance(b, int) or b + k >= 2 * GROUP:
                    act.wait_ge(adj_done, b + (k - GROUP))
                else:
                    act.wait_ge(consts_set, 3)
                loaded(act, at_loaded, b, k)
                act.activation(s_rhs[:, i, :, P:P + 1], at_in[:, i, :, 0:1],
                               ACT.Copy).then_inc(w_col_ready, GROUP)

            def keep_adj(b, k):
                made(act, adj_done, b, k)
                act.activation(adj_sb[:, k % 8], bank_adj[:, 0:2 * P + 2],
                               ACT.Copy).then_inc(adj_kept, 1)

            def round_xt(b, k):
                if first(b, k):
                    act.wait_ge(x0_loaded, 16)
                else:
                    loaded(act, xt_loaded, b, k)
                freed(act, l0_projected, b, k)
                act.activation(xt_hi[:, k % 2], xt_in[:, k // GROUP % 2, k % GROUP],
                               ACT.Copy).then_inc(xt_rounded, 1)

            def keep_pb(b, k):
                made(act, l0_projected, b, k)
                freed(act, l0_done, b, k)
                act.activation(pb_sb[:, k % 2], bank_l0[:, F:2 * F], ACT.Copy).then_inc(pb_kept, 1)

            def round_z(b, k):
                made(act, sx_done, b, k)
                freed(act, conv1_done, b, k)
                act.activation(z_hi[:, k % 2], bank_agg[:, 0:KT * P], ACT.Copy).then_inc(z_rounded, 1)

            def relu_u(b, k):
                made(act, u_ready, b, k)
                freed(act, normed["l1a"], b, k)
                act.activation(h[:, k % 2], u[:, k % 2], ACT.Relu).then_inc(h_relu, 1)

            def keep_sh(b, k):
                made(act, sh_done, b, k)
                freed(act, conv2_done, b, k)
                act.activation(sh_t[:, k % 2], bank_sh[:], ACT.Copy).then_inc(sh_kept, 1)

            def base_beta(b, k):
                pair_made(act, dn_rowsum_ready, b, k)
                if first(b, k):
                    act.wait_ge(rows_kept, 1)
                freed(act, base_b_ready, b, k)
                act.activation(base_a[:, k % 2], w2_beta_row[:], ACT.Copy,
                               scale=dn_rowsum[:, k % 8:k % 8 + 1]).then_inc(base_a_ready, 1)

            def keep_ax(b, k):
                made(act, ax_done, b, k)
                freed(act, l2_done, b, k)
                act.activation(ax_t[:, k % 2], bank_agg[:, 0:KT * P], ACT.Copy).then_inc(ax_kept, 1)

            def exp_att(b, k):
                r = k % 2
                made(act, nm_att_ready, b, k)
                freed(act, att_ready, b, k)
                act.activation(p_att[:, r], em_att[:, r], ACT.Exp, bias=nm_att[:, r:r + 1],
                               accum_out=sum_att[:, r:r + 1]).then_inc(p_att_ready, 1)

            def keep_ax3(b, k):
                made(act, ax3_done, b, k)
                freed(act, l3_done, b, k)
                act.activation(ax3_t[:, k % 2], bank_l2[:, 0:KT * P], ACT.Copy).then_inc(ax3_kept, 1)

            def minus_one(b, k):
                made(act, normed["l2"], b, k)
                freed(act, elu_x_ready, b, k)
                act.activation(x3_m1[:, k % 2], x3[:, k % 2], ACT.Copy, bias=-1.0)\
                    .then_inc(x3_m1_ready, 1)

            def exp_elu(b, k):
                made(act, l3_done, b, k)
                freed(act, y_ready["l3"], b, k)
                act.activation(exp_h[:, k % 2], bank_l3[:, 0:F], ACT.Exp).then_inc(exp_ready, 1)

            def relu_elu(b, k):
                made(act, l3_done, b, k)
                freed(act, elu_x_ready, b, k)
                act.activation(relu_h[:, k % 2], bank_l3[:, 0:F], ACT.Relu).then_inc(relu_h_ready, 1)

            def means(b, k, n):
                r = k % 2
                made(act, y_ready[n], b, k)
                freed(act, normed[n], b, k)
                act.activation(mean_var[n][:, r, 0:1], y_sum[n][:, r:r + 1], ACT.Copy,
                               scale=(1.0 if n == "l0" else -1.0) / F)
                act.activation(shift[n][:, r:r + 1], y_sum[n][:, r:r + 1], ACT.Copy,
                               scale=-ROOT / F).then_inc(means_ready[n], 1)

            def variance(b, k, n):
                r = k % 2
                made(act, means_ready[n], b, k)
                act.activation(squares[n][:, r], Y[n][:, r], ACT.Square, scale=ROOT,
                               bias=shift[n][:, r:r + 1],
                               accum_out=mean_var[n][:, r, 1:2]).then_inc(moments_ready[n], 1)

            def shift_l3(b, k):
                r = k % 2
                made(act, rstd_ready["l3"], b, k)
                act.activation(shift_std[:, r:r + 1], mean_var["l3"][:, r, 0:1], ACT.Copy,
                               scale=rstd["l3"][:, r:r + 1]).then_inc(shift_std_ready, 1)

            def norm_l3(b, k):
                r, i, j = k % 2, k // GROUP % 2, k % GROUP
                made(act, shift_std_ready, b, k)
                if j == 0:
                    act.wait_ge(stored[i], b * 2 + (k // UNROLL * 16 + 16))
                act.activation(out_st[:, i, j], y3[:, r], ACT.Identity, scale=rstd["l3"][:, r:r + 1],
                               bias=shift_std[:, r:r + 1]).then_inc(normed["l3"], 1)

            def step(b, k):
                stage(exp_elu, b, k, 6)
                stage(base_beta, b, k, 3)
                stage_group(edge_weights, b, k, 0)
                stage(relu_elu, b, k, 6)
                stage(round_xt, b, k, 0)
                stage_once(round_w0, b, k, 0, 0)
                stage(keep_sh, b, k, 3)
                stage(relu_u, b, k, 2)
                stage_once(round_w1, b, k, 1)
                stage(means, b, k, 1, "l0")
                stage(keep_ax, b, k, 4)
                stage(variance, b, k, 1, "l0")
                stage(exp_att, b, k, 5)
                stage(means, b, k, 6, "l3")
                stage(variance, b, k, 6, "l3")
                stage_once(round_w0, b, k, 0, 1)
                stage(keep_ax3, b, k, 5)
                stage(round_z, b, k, 1)
                stage(minus_one, b, k, 5)
                stage(keep_pb, b, k, 0)
                stage(shift_l3, b, k, 6)
                stage(keep_adj, b, k, 0)
                stage(norm_l3, b, k, 6)
            run(act, step)

        @block.vector
        def _(dve):
            def stats_of(b, k, n):
                r = k % 2
                made(dve, y_ready[n], b, k)
                freed(dve, moments_ready[n], b, k)
                dve.bn_stats(stats[n][:, r], Y[n][:, r]).then_inc(stats_ready[n], 1)

            def moments(b, k, n):
                plain(dve)
                made(dve, stats_ready[n], b, k)
                dve.bn_aggr(mean_var[n][:, k % 2], stats[n][:, k % 2]).then_inc(moments_ready[n], 1)

            def norm_apply(n, dst, b, k):
                r = k % 2
                dve.tensor_scalar(dst, Y[n][:, r], mean_var[n][:, r, 0:1], rstd[n][:, r:r + 1],
                                  ALU.subtract, ALU.mult).then_inc(normed[n], 1)

            dve.memset(minus_half[:], -0.5).then_inc(consts_set, 1)
            for i in range(2):
                dve.memset(out_st[:, i, 0, 0:1], 0.0).then_inc(stored[i], 16)
            dve.memset(eps_col[:], EPS_LN).then_inc(consts_set, 1)
            dve.memset(s_rhs[:, :, :, P + 1:P + 2], 1.0).then_inc(consts_set, 1)

            def split_w0(c):
                dve.wait_ge(w0_rounded, c + 1)
                dve.tensor_tensor(w0_lo[:, c], w0_raw[:, c], w0_hi[:, c].bitcast(F32), ALU.subtract)\
                    .then_inc(w0_split, 1)

            def split_w1():
                dve.wait_ge(w1_rounded, 1)
                dve.tensor_tensor(w1_lo[:], w1_raw[:], w1_hi[:].bitcast(F32), ALU.subtract)\
                    .then_inc(w1_split, 1)

            def scale_w2():
                dve.wait_ge(late_loads, 16 * LATE)
                for c in range(HT):
                    ins = dve.tensor_scalar(w2_gamma[:, c], w2_raw[:, c], gamma_col[:, c:c + 1], None,
                                            ALU.mult)
                ins.then_inc(w2_scaled, 1)

            def keep_rows():
                dve.wait_ge(rows_made, 1)
                dve.tensor_copy(w2_beta_row[:], bank_conv2[:, 0:F])
                dve.tensor_copy(wa_row[:, 0], bank_l2[:, 0:F])
                dve.tensor_copy(wa_row[:, 1], bank_l3[:, 0:F]).then_inc(rows_kept, 1)

            def degrees(b, k):
                i = k // GROUP % 2
                loaded(dve, a_loaded, b, k)
                dve.tensor_reduce(deg[:, i], a_in[:, i], AX.X, ALU.add).then_inc(deg_sum, GROUP)

            def degree_scales(b, k):
                i = k // GROUP % 2
                group_made(dve, deg_sum, b, k)
                dve.tensor_scalar(deg_max[:, i], deg[:, i], EPS_DEG, None, ALU.max)\
                    .then_inc(deg_clamped, GROUP)
                dve.reciprocal(deg_raw_inv[:, i], deg[:, i]).then_inc(deg_raw_inverted, GROUP)
                group_made(dve, deg_clamped, b, k)
                dve.reciprocal(deg_inv[:, i], deg_max[:, i]).then_inc(deg_inverted, GROUP)
                group_made(dve, deg_raw_inverted, b, k)
                dve.tensor_tensor(deg_ratio[:, i], deg_max[:, i], deg_raw_inv[:, i], ALU.mult)\
                    .then_inc(ratio_ready, GROUP)

            def incidence(b, k):
                i = k // GROUP % 2
                loaded(dve, at_loaded, b, k)
                if not isinstance(b, int) or b + k >= 2 * GROUP:
                    dve.wait_ge(adj_done, b + (k - GROUP))
                dve.tensor_scalar(h_t[:, i], at_in[:, i], 0.0, None, ALU.not_equal)\
                    .then_inc(h_ready, GROUP)

            def count_edges(b, k):
                i = k // GROUP % 2
                group_made(dve, h_ready, b, k)
                dve.tensor_reduce(edge_n[:, i], h_t[:, i], AX.X, ALU.add)\
                    .then_inc(edges_counted, GROUP)

            def edge_scale(b, k):
                i = k // GROUP % 2
                group_made(dve, edges_counted, b, k)
                dve.tensor_scalar(edge_n1[:, i], edge_n[:, i], 1.0, None, ALU.max)\
                    .then_inc(edges_clamped, GROUP)
                group_made(dve, edges_clamped, b, k)
                dve.reciprocal(edge_inv[:, i], edge_n1[:, i]).then_inc(edges_inverted, GROUP)

            def masks(b, k):
                i = k // GROUP % 2
                dve.tensor_scalar(mask[:, i], at_in[:, i], 0.5, None, ALU.is_gt)\
                    .then_inc(mask_ready, GROUP)
                dve.tensor_scalar(penalty[:, i], at_in[:, i], 0.5, NEG_INF, ALU.is_le, ALU.mult)\
                    .then_inc(penalty_ready, GROUP)

            def node_scale(b, k):
                s = k % 8 - 1
                raw = adj_sb[:, s:s + 2, 2 * P]
                made(dve, adj_kept, b, k)
                dve.tensor_scalar(dn_max[:, s:s + 2], raw, TINY, None, ALU.max).then_inc(dn_clamped, 2)
                pair_made(dve, dn_clamped, b, k)
                dve.reciprocal(dn_rec[:, s:s + 2], dn_max[:, s:s + 2]).then_inc(dn_inverted, 2)
                pair_made(dve, dn_inverted, b, k)
                dve.scalar_tensor_tensor(out=dn[:, s:s + 2], in0=raw, scalar=0.0, in1=dn_rec[:, s:s + 2],
                                         op0=ALU.is_gt, op1=ALU.mult).then_inc(dn_ready, 2)
                pair_made(dve, dn_ready, b, k)
                dve.tensor_tensor(dn_rowsum[:, s:s + 2], dn[:, s:s + 2], adj_sb[:, s:s + 2, 2 * P + 1],
                                  ALU.mult).then_inc(dn_rowsum_ready, 2)

            def l0_residual(b, k):
                r = k % 2
                made(dve, l0_done, b, k)
                loaded(dve, x_loaded, b, k)
                freed(dve, normed["l0"], b, k)
                dve.scalar_tensor_tensor(out=y0[:, r], in0=bank_l0[:, 0:F], scalar=0.0,
                                         in1=x_in[:, k // GROUP % 2, k % GROUP],
                                         op0=ALU.max, op1=ALU.add,
                                         accum_out=y_sum["l0"][:, r:r + 1])\
                    .then_inc(y_ready["l0"], 1)

            def l0_norm(b, k):
                made(dve, rstd_ready["l0"], b, k)
                freed(dve, sx_done, b, k)
                freed(dve, base_c_ready, b, k)
                norm_apply("l0", x1[:, k % 2], b, k)

            def split_z(b, k):
                r = k % 2
                made(dve, z_rounded, b, k)
                freed(dve, conv1_done, b, k)
                dve.tensor_tensor(z_lo[:, r], bank_agg[:, 0:KT * P], z_hi[:, r].bitcast(F32),
                                  ALU.subtract).then_inc(z_split, 1)

            def conv1_bias(b, k):
                r, s = k % 2, k % 8
                made(dve, conv1_done, b, k)
                pair_made(dve, dn_ready, b, k)
                freed(dve, h_relu, b, k)
                if first(b, k):
                    dve.wait_ge(late_loads, 16 * LATE)
                dve.scalar_tensor_tensor(out=u[:, r], in0=bank_conv1[:], scalar=dn[:, s:s + 1],
                                         in1=b1_row[:], op0=ALU.mult, op1=ALU.add)\
                    .then_inc(u_ready, 1)

            def l1a_norm(b, k):
                made(dve, rstd_ready["l1a"], b, k)
                freed(dve, sh_done, b, k)
                norm_apply("l1a", hn[:, k % 2], b, k)

            def l1_residual(b, k):
                r, s = k % 2, k % 8
                made(dve, conv2_done, b, k)
                made(dve, base_ready, b, k)
                freed(dve, normed["l1b"], b, k)
                dve.scalar_tensor_tensor(out=y1[:, r], in0=bank_conv2[:, 0:F], scalar=dn[:, s:s + 1],
                                         in1=base[:, r], op0=ALU.mult, op1=ALU.add)\
                    .then_inc(y_ready["l1b"], 1)

            def l1b_norm(b, k):
                made(dve, rstd_ready["l1b"], b, k)
                freed(dve, ax_done, b, k)
                freed(dve, x2_b_ready, b, k)
                norm_apply("l1b", x2[:, k % 2], b, k)

            def l2_residual(b, k):
                r = k % 2
                made(dve, l2_done, b, k)
                made(dve, x2_b_ready, b, k)
                freed(dve, normed["l2"], b, k)
                dve.scalar_tensor_tensor(out=y2[:, r], in0=bank_l2[:, 0:F],
                                         scalar=deg_ratio_ring[:, k % 8:k % 8 + 1],
                                         in1=x2_b[:, r], op0=ALU.mult, op1=ALU.add)\
                    .then_inc(y_ready["l2"], 1)

            deg_ratio_ring = deg_ratio[:].rearrange("p i j -> p (i j)")

            def l2_norm(b, k):
                made(dve, rstd_ready["l2"], b, k)
                freed(dve, ax3_done, b, k)
                freed(dve, x3_m1_ready, b, k)
                norm_apply("l2", x3[:, k % 2], b, k)

            def node_scores(b, k, a, ready):
                r = k % 2
                made(dve, normed["l2"], b, k)
                freed(dve, (src_done, z_att_ready)[a], b, k)
                dve.tensor_tensor_reduce(junk[:, r, a], x3[:, r], wa_row[:, a], 1.0, 0.0,
                                         ALU.mult, ALU.add, wh[:, r, a:a + 1]).then_inc(ready, 1)

            def src_weight(b, k):
                node_scores(b, k, 0, wh1_ready)

            def dst_weight(b, k):
                node_scores(b, k, 1, wh2_ready)

            def scores(b, k):
                r, i, j = k % 2, k // GROUP % 2, k % GROUP
                made(dve, src_done, b, k)
                made(dve, wh2_ready, b, k)
                group_made(dve, mask_ready, b, k)
                freed(dve, p_att_ready, b, k)
                dve.scalar_tensor_tensor(out=z_att[:, r], in0=bank_adj[:, 0:P], scalar=wh[:, r, 1:2],
                                         in1=mask[:, i, j], op0=ALU.add, op1=ALU.mult)\
                    .then_inc(z_att_ready, 1)

            def leaky(b, k):
                r = k % 2
                made(dve, z_att_ready, b, k)
                dve.scalar_tensor_tensor(out=e_att[:, r], in0=z_att[:, r], scalar=ALPHA,
                                         in1=z_att[:, r], op0=ALU.mult, op1=ALU.max)\
                    .then_inc(e_att_ready, 1)

            def masked(b, k):
                r, i, j = k % 2, k // GROUP % 2, k % GROUP
                plain(dve)
                made(dve, e_att_ready, b, k)
                dve.tensor_tensor_reduce(em_att[:, r], e_att[:, r], penalty[:, i, j], 1.0, LOWEST,
                                         ALU.add, ALU.max, m_att[:, r:r + 1]).then_inc(em_att_ready, 1)

            def neg_max(b, k):
                r = k % 2
                made(dve, em_att_ready, b, k)
                dve.tensor_scalar(nm_att[:, r:r + 1], m_att[:, r:r + 1], -1.0, None, ALU.mult)\
                    .then_inc(nm_att_ready, 1)

            def att_inv(b, k):
                r = k % 2
                made(dve, p_att_ready, b, k)
                dve.reciprocal(inv_att[:, r:r + 1], sum_att[:, r:r + 1]).then_inc(inv_att_ready, 1)

            def attention(b, k):
                r = k % 2
                made(dve, inv_att_ready, b, k)
                freed(dve, ax3_done, b, k)
                dve.tensor_scalar(att_t[:, r], p_att[:, r], inv_att[:, r:r + 1], None, ALU.mult)\
                    .then_inc(att_ready, 1)

            def l3_residual(b, k):
                r = k % 2
                made(dve, elu_x_ready, b, k)
                made(dve, exp_ready, b, k)
                freed(dve, normed["l3"], b, k)
                dve.scalar_tensor_tensor(out=y3[:, r], in0=exp_h[:, r], scalar=1.0, in1=elu_x[:, r],
                                         op0=ALU.min, op1=ALU.add,
                                         accum_out=y_sum["l3"][:, r:r + 1])\
                    .then_inc(y_ready["l3"], 1)

            def step(b, k):
                stage_group(incidence, b, k, 0)
                stage(neg_max, b, k, 6)
                stage_once(split_w0, b, k, 1, 1)
                stage(stats_of, b, k, 3, "l1a")
                stage_group(count_edges, b, k, 0)
                stage_group(degree_scales, b, k, 1)
                stage(att_inv, b, k, 6)
                stage(moments, b, k, 3, "l1a")
                stage_group(edge_scale, b, k, 0)
                stage_once(scale_w2, b, k, 2)
                stage(attention, b, k, 6)
                stage(l2_residual, b, k, 5)
                stage(l0_norm, b, k, 2)
                stage(stats_of, b, k, 5, "l2")
                stage(l1_residual, b, k, 4)
                stage_once(split_w1, b, k, 2)
                stage(moments, b, k, 5, "l2")
                stage(l1a_norm, b, k, 3)
                stage(stats_of, b, k, 4, "l1b")
                stage(split_z, b, k, 2)
                stage(moments, b, k, 4, "l1b")
                stage(l2_norm, b, k, 5)
                stage_pair(node_scale, b, k, 1)
                stage_once(keep_rows, b, k, 3)
                stage(src_weight, b, k, 5)
                stage(l1b_norm, b, k, 4)
                stage_group(masks, b, k, 3)
                stage(dst_weight, b, k, 5)
                stage(conv1_bias, b, k, 2)
                stage_once(split_w0, b, k, 1, 0)
                stage(scores, b, k, 5)
                stage(l0_residual, b, k, 1)
                stage(leaky, b, k, 5)
                stage(l3_residual, b, k, 6)
                stage(masked, b, k, 5)
                stage_group(degrees, b, k, 0)
            run(dve, step)

        @block.gpsimd
        def _(pool):
            def add_eps(b, k, n):
                r = k % 2
                made(pool, moments_ready[n], b, k)
                freed(pool, normed[n], b, k)
                pool.tensor_tensor(var_eps[n][:, r:r + 1], mean_var[n][:, r, 1:2], eps_col[:],
                                   ALU.add).then_inc(var_eps_ready[n], 1)

            def power(b, k, n):
                r = k % 2
                made(pool, var_eps_ready[n], b, k)
                pool.tensor_tensor(rstd[n][:, r:r + 1], var_eps[n][:, r:r + 1], minus_half[:],
                                   ALU.pow).then_inc(rstd_ready[n], 1)

            def scale_group(b, k):
                i = k // GROUP % 2
                group_made(pool, deg_inverted, b, k)
                if not isinstance(b, int) or b + k >= 2 * GROUP:
                    pool.wait_ge(adj_done, b + (k - GROUP))
                pool.tensor_tensor(a_norm[:, i], a_in[:, i],
                                   deg_inv[:, i].unsqueeze(2).to_broadcast([P, GROUP, P]),
                                   ALU.mult).then_inc(a_normed, GROUP)

            def scale_edges(b, k):
                i = k // GROUP % 2
                group_made(pool, edges_inverted, b, k)
                pool.tensor_tensor(s_rhs[:, i, :, 0:P], h_t[:, i],
                                   edge_inv[:, i].unsqueeze(2).to_broadcast([P, GROUP, P]),
                                   ALU.mult).then_inc(s_rhs_ready, GROUP)

            def split_xt(b, k):
                r = k % 2
                made(pool, xt_rounded, b, k)
                freed(pool, l0_projected, b, k)
                pool.tensor_tensor(xt_lo[:, r], xt_in[:, k // GROUP % 2, k % GROUP],
                                   xt_hi[:, r].bitcast(F32), ALU.subtract).then_inc(xt_split, 1)

            def base_bias(b, k):
                r = k % 2
                made(pool, base_a_ready, b, k)
                freed(pool, base_ready, b, k)
                if first(b, k):
                    pool.wait_ge(late_loads, 16 * LATE)
                pool.tensor_tensor(base_b[:, r], base_a[:, r], b2_row[:], ALU.add)\
                    .then_inc(base_b_ready, 1)

            def base_double(b, k):
                r = k % 2
                plain(pool)
                made(pool, normed["l0"], b, k)
                freed(pool, base_ready, b, k)
                pool.tensor_scalar(base_c[:, r], x1[:, r], 2.0, 0.0, ALU.mult, ALU.add)\
                    .then_inc(base_c_ready, 1)

            def base_sum(b, k):
                r = k % 2
                made(pool, base_b_ready, b, k)
                made(pool, base_c_ready, b, k)
                freed(pool, y_ready["l1b"], b, k)
                pool.tensor_tensor(base[:, r], base_b[:, r], base_c[:, r], ALU.add)\
                    .then_inc(base_ready, 1)

            def elu_sum(b, k):
                r = k % 2
                made(pool, relu_h_ready, b, k)
                made(pool, x3_m1_ready, b, k)
                freed(pool, y_ready["l3"], b, k)
                pool.tensor_tensor(elu_x[:, r], relu_h[:, r], x3_m1[:, r], ALU.add)\
                    .then_inc(elu_x_ready, 1)

            def l2_bias(b, k):
                made(pool, normed["l1b"], b, k)
                freed(pool, y_ready["l2"], b, k)
                pool.tensor_tensor(x2_b[:, k % 2], x2[:, k % 2], bl2_row[:], ALU.add)\
                    .then_inc(x2_b_ready, 1)

            def step(b, k):
                if first(b, k):
                    pool.wait_ge(consts_set, 3)
                stage_group(scale_edges, b, k, 0)
                stage(add_eps, b, k, 5, "l2")
                stage(power, b, k, 5, "l2")
                stage(add_eps, b, k, 4, "l1b")
                stage(power, b, k, 4, "l1b")
                stage(base_bias, b, k, 3)
                stage(base_double, b, k, 3)
                stage(elu_sum, b, k, 6)
                stage(l2_bias, b, k, 4)
                stage(split_xt, b, k, 0)
                stage(base_sum, b, k, 3)
                stage(add_eps, b, k, 1, "l0")
                stage(power, b, k, 1, "l0")
                stage(add_eps, b, k, 2, "l1a")
                stage_group(scale_group, b, k, 0)
                stage(add_eps, b, k, 6, "l3")
                stage(power, b, k, 2, "l1a")
                stage(power, b, k, 6, "l3")
            run(pool, step)


def kernel(x, adj, L0_gnn_W, L1_gnn_W1, L1_gnn_b1, L1_gnn_gamma, L1_gnn_beta, L1_gnn_W2, L1_gnn_b2,
           L2_gnn_W, L2_gnn_b, L3_gnn_W, L3_gnn_a):
    import numpy as np
    import concourse.bacc as bacc
    from concourse.bass_utils import run_bass_kernel_spmd

    x, adj = np.asarray(x), np.asarray(adj)
    n, p, f = x.shape
    groups, kt = n // GROUP, f // p

    def rows(w):
        w = np.asarray(w)
        return w.reshape(w.shape[0] // p, p, w.shape[1]).transpose(1, 0, 2)

    def cols(v):
        return np.asarray(v).reshape(-1, p).T

    w0, w3 = np.asarray(L0_gnn_W), np.asarray(L3_gnn_W)
    arrays = {
        "x_nodes": x.reshape(groups, GROUP, p, f).transpose(0, 2, 1, 3),
        "x_feats": x.reshape(groups, GROUP, p, kt, p).transpose(0, 4, 1, 3, 2),
        "adj_rows": adj.reshape(groups, GROUP, p, p).transpose(0, 2, 1, 3),
        "adj_cols": adj.reshape(groups, GROUP, p, p).transpose(0, 3, 1, 2),
        "ident": np.eye(p, dtype=x.dtype),
        "w0_t": rows(np.concatenate([w0[:, :f].T, w0[:, f:].T], axis=1)),
        "w1_t": rows(np.asarray(L1_gnn_W1).T),
        "b1": np.asarray(L1_gnn_b1),
        "gamma": cols(L1_gnn_gamma),
        "beta": cols(L1_gnn_beta),
        "w2_t": rows(np.asarray(L1_gnn_W2).T),
        "b2": np.asarray(L1_gnn_b2),
        "w_l2": rows(L2_gnn_W),
        "b_l2": np.asarray(L2_gnn_b),
        "w_l3": rows(w3),
        "w_l3_t": rows(w3.T),
        "attn": cols(L3_gnn_a),
    }
    nc = bacc.Bacc("TRN2", target_bir_lowering=False, num_devices=1)
    ins, args = {}, []
    for name, a in arrays.items():
        a = np.ascontiguousarray(a)
        ins[f"in_{name}"] = a
        args.append(nc.dram_tensor(f"in_{name}", a.shape, mybir.dt.from_np(a.dtype),
                                   kind="ExternalInput").ap())
    out = nc.dram_tensor("out_x", (groups, p, GROUP, f), F32, kind="ExternalOutput").ap()
    build(nc, *args, out)
    r = run_bass_kernel_spmd(nc, [ins], core_ids=[0])
    got = r.results[0]["out_x"]
    return np.ascontiguousarray(got.transpose(0, 2, 1, 3)).reshape(n, p, f)
```

```python
from contextlib import ExitStack

import concourse.bass as bass
from concourse import mybir

ALU = mybir.AluOpType
ACT = mybir.ActivationFunctionType
AX = mybir.AxisListType
F32 = mybir.dt.float32
F32R = mybir.dt.float32r

EPS_DEG = 1e-6
EPS_LN = 1e-5
ALPHA = 0.2
NEG_INF = -9000000000000000.0
TINY = 1.1754944e-38
LOWEST = -3.0e38

GROUP = 4
UNROLL = 8
PEELED = 2 * UNROLL

def build(nc, x, x_t, adj, adj_t, ident, w0_t, w1_t, b1, gamma, beta, w2_t, b2, w_l2, b_l2,
          w_l3, w_l3_t, attn, degrees_dram, out):
    G, P, _, F = x.shape
    GRAPHS = G * GROUP
    KT = F // P
    H = w1_t.shape[2]
    HT = H // P
    DRAIN = 7

    with ExitStack() as ctx:
        def sb(name, shape, dt=F32):
            return ctx.enter_context(nc.sbuf_tensor(name, shape, dt))

        def bank(name):
            return ctx.enter_context(nc.psum_tensor(name, [P, 512], F32))

        def sem(name):
            return ctx.enter_context(nc.semaphore(name))

        identity = sb("identity", [P, P])
        w0_raw = sb("w0_raw", [P, KT, 2 * F])
        w0_hi = sb("w0_hi", [P, KT, 2 * F], F32R)
        w0_lo = sb("w0_lo", [P, KT, 2 * F], F32R)
        w1_raw = sb("w1_raw", [P, KT, H])
        w1_hi = sb("w1_hi", [P, KT, H], F32R)
        w1_lo = sb("w1_lo", [P, KT, H], F32R)
        w2_raw = sb("w2_raw", [P, HT, F])
        w2_gamma = sb("w2_gamma", [P, HT, F])
        w2_hi = sb("w2_hi", [P, HT, F], F32R)
        w2_lo = sb("w2_lo", [P, HT, F], F32R)
        wl2 = sb("wl2", [P, KT, F])
        wl3 = sb("wl3", [P, KT, F])
        wl3_t = sb("wl3_t", [P, KT, F])
        b1_row = sb("b1_row", [P, H])
        b2_row = sb("b2_row", [P, F])
        bl2_row = sb("bl2_row", [P, F])
        gamma_col = sb("gamma_col", [P, HT])
        beta_col = sb("beta_col", [P, HT])
        attn_col = sb("attn_col", [P, 2 * KT])
        w2_beta_row = sb("w2_beta_row", [P, F])
        wa_row = sb("wa_row", [P, 2, F])
        eps_col = sb("eps_col", [P, 1])
        minus_half = sb("minus_half", [P, 1])

        x_in = sb("x_in", [P, 2, GROUP, F])
        xt_in = sb("xt_in", [P, 2, GROUP, KT, P])
        a_in = sb("a_in", [P, 2, GROUP, P])
        at_in = sb("at_in", [P, 2, GROUP, P])
        out_st = sb("out_st", [P, 2, GROUP, F])

        deg = sb("deg", [P, 2, GROUP])
        deg_max = sb("deg_max", [P, 2, GROUP])
        deg_inv = sb("deg_inv", [P, 2, GROUP])
        deg_raw_inv = sb("deg_raw_inv", [P, 2, GROUP])
        deg_ratio = sb("deg_ratio", [P, 2, GROUP])
        deg_row = sb("deg_row", [P, 2, P, GROUP])
        an_t = sb("an_t", [P, 2, GROUP, P])
        h_t = sb("h_t", [P, 2, GROUP, P])
        edge_n = sb("edge_n", [P, 2, GROUP])
        edge_n1 = sb("edge_n1", [P, 2, GROUP])
        edge_inv = sb("edge_inv", [P, 2, GROUP])
        s_rhs = sb("s_rhs", [P, 2, GROUP, P + 2])
        mask = sb("mask", [P, 2, GROUP, P])
        penalty = sb("penalty", [P, 2, GROUP, P])
        adj_sb = sb("adj_sb", [P, 8, P + 2])
        dn_max = sb("dn_max", [P, 8])
        dn_rec = sb("dn_rec", [P, 8])
        dn = sb("dn", [P, 8])
        dn_rowsum = sb("dn_rowsum", [P, 8])

        xt_hi = sb("xt_hi", [P, 2, KT, P], F32R)
        xt_lo = sb("xt_lo", [P, 2, KT, P], F32R)
        pb_sb = sb("pb_sb", [P, 2, F])
        y0 = sb("y0", [P, 2, F])
        x1 = sb("x1", [P, 2, F])
        z_hi = sb("z_hi", [P, 2, KT * P], F32R)
        z_lo = sb("z_lo", [P, 2, KT * P], F32R)
        u = sb("u", [P, 2, H])
        h = sb("h", [P, 2, H])
        hn = sb("hn", [P, 2, H])
        sh_hi = sb("sh_hi", [P, 2, HT * P], F32R)
        sh_lo = sb("sh_lo", [P, 2, HT * P], F32R)
        base_a = sb("base_a", [P, 2, F])
        base_b = sb("base_b", [P, 2, F])
        base_c = sb("base_c", [P, 2, F])
        base = sb("base", [P, 2, F])
        y1 = sb("y1", [P, 2, F])
        x2 = sb("x2", [P, 2, F])
        x2_b = sb("x2_b", [P, 2, F])
        ax_t = sb("ax_t", [P, 2, KT * P])
        y2 = sb("y2", [P, 2, F])
        x3 = sb("x3", [P, 2, F])
        junk = sb("junk", [P, 2, 2, F])
        wh = sb("wh", [P, 2, 2])
        z_att = sb("z_att", [P, 2, P])
        e_att = sb("e_att", [P, 2, P])
        em_att = sb("em_att", [P, 2, P])
        m_att = sb("m_att", [P, 2])
        nm_att = sb("nm_att", [P, 2])
        p_att = sb("p_att", [P, 2, P])
        sum_att = sb("sum_att", [P, 2])
        inv_att = sb("inv_att", [P, 2])
        att_t = sb("att_t", [P, 2, P])
        ax3_t = sb("ax3_t", [P, 2, KT * P])
        exp_h = sb("exp_h", [P, 2, F])
        relu_h = sb("relu_h", [P, 2, F])
        elu_x = sb("elu_x", [P, 2, F])
        y3 = sb("y3", [P, 2, F])
        NORMS = ("l0", "l1a", "l1b", "l2", "l3")
        WIDTH = {n: H if n == "l1a" else F for n in NORMS}
        ACT_NORMS = ("l0", "l1a", "l1b", "l3")
        DVE_NORMS = tuple(n for n in NORMS if n not in ACT_NORMS)
        stats = {n: sb(f"stats_{n}", [P, 2, 6]) for n in DVE_NORMS}
        mean_var = {n: sb(f"mean_var_{n}", [P, 2, 2]) for n in NORMS}
        var_eps = {n: sb(f"var_eps_{n}", [P, 2]) for n in NORMS}
        y_sum = {n: sb(f"y_sum_{n}", [P, 2]) for n in ACT_NORMS}
        shift = {n: sb(f"shift_{n}", [P, 2]) for n in ACT_NORMS}
        squares = {n: sb(f"squares_{n}", [P, 2, WIDTH[n]]) for n in ACT_NORMS}
        shift_std = sb("shift_std", [P, 2])
        rstd = {n: sb(f"rstd_{n}", [P, 2]) for n in NORMS}

        bank_l0 = bank("bank_l0")
        bank_conv1 = bank("bank_conv1")
        bank_sh = bank("bank_sh")
        bank_conv2 = bank("bank_conv2")
        bank_agg = bank("bank_agg")
        bank_l2 = bank("bank_l2")
        bank_l3 = bank("bank_l3")
        bank_adj = bank("bank_adj")

        ident_loaded = sem("ident_loaded")
        w0_loaded = [sem(f"w0_loaded{c}") for c in range(KT)]
        x0_loaded = sem("x0_loaded")
        w1_loaded = sem("w1_loaded")
        late_loads = sem("late_loads")
        consts_set = sem("consts_set")
        w0_rounded = sem("w0_rounded")
        w1_rounded = sem("w1_rounded")
        w0_split = sem("w0_split")
        w1_split = sem("w1_split")
        w2_scaled = sem("w2_scaled")
        w2_rounded = sem("w2_rounded")
        w2_split = sem("w2_split")
        rows_made = sem("rows_made")
        rows_kept = sem("rows_kept")
        x_loaded = [sem(f"x_loaded{i}") for i in range(2)]
        xt_loaded = [sem(f"xt_loaded{i}") for i in range(2)]
        a_loaded = [sem(f"a_loaded{i}") for i in range(2)]
        at_loaded = [sem(f"at_loaded{i}") for i in range(2)]
        degree_rows_made = sem("degree_rows_made")
        deg_stored = sem("deg_stored")
        deg_row_loaded = [sem(f"deg_row_loaded{i}") for i in range(2)]
        stored = [sem(f"stored{i}") for i in range(2)]
        deg_sum = sem("deg_sum")
        deg_clamped = sem("deg_clamped")
        deg_inverted = sem("deg_inverted")
        deg_raw_inverted = sem("deg_raw_inverted")
        ratio_ready = sem("ratio_ready")
        an_ready = sem("an_ready")
        h_ready = sem("h_ready")
        edges_counted = sem("edges_counted")
        edges_clamped = sem("edges_clamped")
        edges_inverted = sem("edges_inverted")
        s_rhs_ready = sem("s_rhs_ready")
        w_col_ready = sem("w_col_ready")
        mask_ready = sem("mask_ready")
        penalty_ready = sem("penalty_ready")
        dn_clamped = sem("dn_clamped")
        dn_inverted = sem("dn_inverted")
        dn_ready = sem("dn_ready")
        dn_rowsum_ready = sem("dn_rowsum_ready")
        adj_done = sem("adj_done")
        adj_kept = sem("adj_kept")
        xt_rounded = sem("xt_rounded")
        xt_split = sem("xt_split")
        l0_projected = sem("l0_projected")
        pb_kept = sem("pb_kept")
        l0_done = sem("l0_done")
        sx_done = sem("sx_done")
        z_rounded = sem("z_rounded")
        z_split = sem("z_split")
        conv1_done = sem("conv1_done")
        u_ready = sem("u_ready")
        h_relu = sem("h_relu")
        sh_done = sem("sh_done")
        sh_rounded = sem("sh_rounded")
        sh_split = sem("sh_split")
        conv2_done = sem("conv2_done")
        base_a_ready = sem("base_a_ready")
        base_b_ready = sem("base_b_ready")
        base_c_ready = sem("base_c_ready")
        base_ready = sem("base_ready")
        x2_b_ready = sem("x2_b_ready")
        ax_done = sem("ax_done")
        ax_kept = sem("ax_kept")
        l2_done = sem("l2_done")
        wh1_ready = sem("wh1_ready")
        wh2_ready = sem("wh2_ready")
        src_done = sem("src_done")
        z_att_ready = sem("z_att_ready")
        e_att_ready = sem("e_att_ready")
        em_att_ready = sem("em_att_ready")
        nm_att_ready = sem("nm_att_ready")
        p_att_ready = sem("p_att_ready")
        inv_att_ready = sem("inv_att_ready")
        att_ready = sem("att_ready")
        ax3_done = sem("ax3_done")
        ax3_kept = sem("ax3_kept")
        l3_done = sem("l3_done")
        exp_ready = sem("exp_ready")
        relu_h_ready = sem("relu_h_ready")
        elu_x_ready = sem("elu_x_ready")
        y_ready = {n: sem(f"y_{n}_ready") for n in NORMS if n != "l1a"}
        stats_ready = {n: sem(f"stats_{n}_ready") for n in DVE_NORMS}
        moments_ready = {n: sem(f"moments_{n}_ready") for n in NORMS}
        var_eps_ready = {n: sem(f"var_eps_{n}_ready") for n in NORMS}
        rstd_ready = {n: sem(f"rstd_{n}_ready") for n in NORMS}
        means_ready = {n: sem(f"means_{n}_ready") for n in ACT_NORMS}
        shift_std_ready = sem("shift_std_ready")
        normed = {n: sem(f"normed_{n}") for n in NORMS}
        y_ready["l1a"] = h_relu
        Y = {"l0": y0, "l1a": h, "l1b": y1, "l2": y2, "l3": y3}

        LATE = 10

        def exists(b, k):
            return not isinstance(b, int) or 0 <= b + k < GRAPHS

        def made(eng, s, b, k):
            eng.wait_ge(s, b + (k + 1))

        def freed(eng, s, b, k, ring=2):
            if isinstance(b, int) and b + k - ring < 0:
                return
            eng.wait_ge(s, b + (k - ring + 1))

        def made_for_plain(eng, s, b, k):
            count = b + (k + 1)
            eng.wait_ge(consts_set, 3)
            eng.wait_ge(s, count)

        def group_made(eng, s, b, k):
            eng.wait_ge(s, b + (k - k % GROUP + GROUP))

        def pair_made(eng, s, b, k):
            eng.wait_ge(s, b + (k - k % 2 + 2))

        def loaded(eng, sems, b, k):
            eng.wait_ge(sems[k // GROUP % 2], b * 2 + (k // UNROLL * 16 + 16))

        def run(eng, step):
            for b in range(0, PEELED, UNROLL):
                for k in range(UNROLL):
                    step(b, k)
            with eng.Fori(PEELED, GRAPHS, UNROLL) as b:
                for k in range(UNROLL):
                    step(b, k)
            for k in range(DRAIN):
                step(GRAPHS, k)

        def first(b, k):
            return isinstance(b, int) and b + k == 0

        def stage(f, b, k, lag, *which):
            if exists(b, k - lag):
                f(b, k - lag, *which)

        def stage_once(f, b, k, lag, *which):
            if first(b, k - lag):
                f(*which)

        def stage_begun(how, f, b, k, lag):
            if not first(b, k - lag):
                how(f, b, k, lag)

        def stage_group(f, b, k, lag):
            if (k - lag) % GROUP == 0:
                stage(f, b, k, lag)

        def stage_pair(f, b, k, lag):
            if (k - lag) % 2 == 1:
                stage(f, b, k, lag)

        block = ctx.enter_context(nc.Block())

        @block.sync
        def _(sp):
            def load_adj(q, i):
                if not (isinstance(q, int) and q == 0):
                    sp.wait_ge(deg_sum, q * UNROLL + (i * GROUP - GROUP))
                    sp.wait_ge(an_ready, q * UNROLL + (i * GROUP - GROUP))
                    sp.wait_ge(h_ready, q * UNROLL + (i * GROUP - GROUP))
                    sp.wait_ge(w_col_ready, q * UNROLL + (i * GROUP - GROUP))
                    sp.wait_ge(penalty_ready, q * UNROLL + (i * GROUP - GROUP))
                sp.dma_start(a_in[:, i], adj[q * 2 + i]).then_inc(a_loaded[i], 16)
                sp.dma_start(at_in[:, i], adj_t[q * 2 + i]).then_inc(at_loaded[i], 16)

            def load_x(q, i):
                if not (isinstance(q, int) and q == 0):
                    sp.wait_ge(xt_split, q * UNROLL + (i * GROUP - GROUP))
                    sp.wait_ge(y_ready["l0"], q * UNROLL + (i * GROUP - GROUP))
                sp.dma_start(xt_in[:, i], x_t[q * 2 + i]).then_inc(xt_loaded[i], 16)
                sp.dma_start(x_in[:, i], x[q * 2 + i]).then_inc(x_loaded[i], 16)

            def turn_degrees(q, i):
                sp.wait_ge(deg_inverted, q * UNROLL + (i * GROUP + GROUP))
                sp.dma_start(degrees_dram[q * 2 + i], deg_inv[:, i]).then_inc(deg_stored, 16)
                sp.wait_ge(deg_stored, q * 32 + i * 16)
                sp.dma_start(deg_row[:, i], degrees_dram[q * 2 + i].partition_broadcast(P))\
                    .then_inc(deg_row_loaded[i], 16)

            def store(q, i):
                sp.wait_ge(normed["l3"], q * UNROLL + (i * GROUP + GROUP))
                sp.dma_start(out[q * 2 + i], out_st[:, i]).then_inc(stored[i], 16)

            sp.dma_start(xt_in[:, 0, 0], x_t[0][:, 0]).then_inc(x0_loaded, 16)
            for c in range(KT):
                sp.dma_start(w0_raw[:, c], w0_t[:, c]).then_inc(w0_loaded[c], 16)
            load_adj(0, 0)
            sp.dma_start(identity[:], ident).then_inc(ident_loaded, 16)
            sp.dma_start(xt_in[:, 0, 1:GROUP], x_t[0][:, 1:GROUP]).then_inc(xt_loaded[0], 16)
            sp.dma_start(x_in[:, 0], x[0]).then_inc(x_loaded[0], 16)
            sp.dma_start(w1_raw[:], w1_t).then_inc(w1_loaded, 16)
            late = ((b1_row[:], b1.partition_broadcast(P)),
                    (gamma_col[:], gamma), (beta_col[:], beta), (attn_col[:], attn),
                    (w2_raw[:], w2_t), (wl3_t[:], w_l3_t),
                    (b2_row[:], b2.partition_broadcast(P)), (wl2[:], w_l2),
                    (bl2_row[:], b_l2.partition_broadcast(P)), (wl3[:], w_l3))
            assert len(late) == LATE
            for dst, src in late:
                sp.dma_start(dst, src).then_inc(late_loads, 16)
            load_adj(0, 1)
            load_x(0, 1)

            def load_block(q):
                for i in range(2):
                    load_adj(q, i)
                    turn_degrees(*((q - 1, 1) if i == 0 else (q, 0)))
                    load_x(q, i)
                    if i == 1 or not isinstance(q, int):
                        store(*((q - 2, 1) if i == 0 else (q - 1, 0)))

            load_block(1)
            with sp.Fori(2, GRAPHS // UNROLL) as q:
                load_block(q)
            last = GRAPHS // UNROLL - 1
            turn_degrees(last, 1)
            store(last - 1, 1)
            for i in range(2):
                store(last, i)
            for i in range(2):
                sp.wait_ge(stored[i], 16 * (G // 2) + 16)

        @block.tensor
        def _(pe):
            def chunk(t, c):
                return t[:, c * P:(c + 1) * P]

            def bank_free(b, k, own, other, ahead):
                if isinstance(b, int):
                    if 0 < b + k:
                        made(pe, own, b, k - 1)
                    if b + k + ahead >= GRAPHS:
                        pe.wait_ge(other, GRAPHS)
                        return
                    if b + k + ahead < 0:
                        return
                made(pe, other, b, k + ahead)

            def constant_rows():
                pe.wait_ge(an_ready, GROUP)
                pe.wait_ge(late_loads, 16 * LATE)
                for c in range(HT):
                    mm = pe.matmul(bank_conv2[:, 0:F], beta_col[:, c:c + 1].to_broadcast([P, P]),
                                   w2_raw[:, c], start=(c == 0), stop=(c == HT - 1))
                for a in range(2):
                    for c in range(KT):
                        col = attn_col[:, a * KT + c:a * KT + c + 1]
                        mm = pe.matmul((bank_l2, bank_l3)[a][:, 0:F], col.to_broadcast([P, P]),
                                       wl3_t[:, c], start=(c == 0), stop=(c == KT - 1))
                mm.then_inc(rows_made, 1)

            def first_degree_rows():
                pe.wait_ge(ident_loaded, 16)
                pe.wait_ge(deg_inverted, GROUP)
                for j in range(GROUP):
                    mm = pe.transpose(bank_l3[:, j * P:(j + 1) * P],
                                      deg_inv[:, 0, j:j + 1].to_broadcast([P, P]), identity[:])
                mm.then_inc(degree_rows_made, 1)

            def adjacency(b, k):
                i, j = k // GROUP % 2, k % GROUP
                group_made(pe, s_rhs_ready, b, k)
                group_made(pe, w_col_ready, b, k)
                bank_free(b, k, adj_kept, z_att_ready, -5)
                pe.matmul(bank_adj[:, 0:P + 2], h_t[:, i, j], s_rhs[:, i, j],
                          start=True, stop=True).then_inc(adj_done, 1)

            def split_product(psum, hi, lo, w_hi, w_lo, ready):
                n = len(hi)
                for c in range(n):
                    pe.matmul(psum, hi[c], w_hi[:, c], start=(c == 0), stop=False)
                    pe.matmul(psum, hi[c], w_lo[:, c], start=False, stop=False)
                for c in range(n):
                    mm = pe.matmul(psum, lo[c], w_hi[:, c], start=False, stop=(c == n - 1))
                mm.then_inc(ready, 1)

            def l0_project(b, k):
                r = k % 2
                made(pe, xt_split, b, k)
                if first(b, k):
                    pe.wait_ge(w0_split, KT)
                freed(pe, y_ready["l0"], b, k, 1)
                split_product(bank_l0[:], [xt_hi[:, r, c] for c in range(KT)],
                              [xt_lo[:, r, c] for c in range(KT)], w0_hi, w0_lo, l0_projected)

            def l0_aggregate(b, k):
                made(pe, pb_kept, b, k)
                group_made(pe, an_ready, b, k)
                pe.matmul(bank_l0[:, 0:F], an_t[:, k // GROUP % 2, k % GROUP], pb_sb[:, k % 2],
                          start=False, stop=True, skip_group_check=True).then_inc(l0_done, 1)

            def aggregate(psum, stationary, moving, n, ready):
                for c in range(n):
                    mm = pe.matmul(chunk(psum, c), chunk(stationary, c), moving,
                                   start=True, stop=True)
                mm.then_inc(ready, 1)

            def product(psum, stationary, w, n, ready):
                for c in range(n):
                    mm = pe.matmul(psum[:, 0:F], chunk(stationary, c), w[:, c],
                                   start=(c == 0), stop=(c == n - 1))
                mm.then_inc(ready, 1)

            def conv1_aggregate(b, k):
                made(pe, normed["l0"], b, k)
                bank_free(b, k, z_split, ax_kept, -3)
                made(pe, adj_kept, b, k)
                aggregate(bank_agg, x1[:, k % 2], adj_sb[:, k % 8, 0:P], KT, sx_done)

            def conv1_product(b, k):
                r = k % 2
                made(pe, z_split, b, k)
                freed(pe, u_ready, b, k, 1)
                if first(b, k):
                    pe.wait_ge(w1_split, 1)
                split_product(bank_conv1[:], [chunk(z_hi[:, r], c) for c in range(KT)],
                              [chunk(z_lo[:, r], c) for c in range(KT)], w1_hi, w1_lo, conv1_done)

            def conv2_aggregate(b, k):
                made(pe, normed["l1a"], b, k)
                freed(pe, sh_split, b, k, 1)
                aggregate(bank_sh, hn[:, k % 2], adj_sb[:, k % 8, 0:P], HT, sh_done)

            def conv2_product(b, k):
                r = k % 2
                made(pe, sh_split, b, k)
                freed(pe, y_ready["l1b"], b, k, 1)
                if first(b, k):
                    pe.wait_ge(w2_split, 1)
                    pe.wait_ge(rows_kept, 1)
                split_product(bank_conv2[:, 0:F], [chunk(sh_hi[:, r], c) for c in range(HT)],
                              [chunk(sh_lo[:, r], c) for c in range(HT)], w2_hi, w2_lo, conv2_done)

            def l2_aggregate(b, k):
                made(pe, normed["l1b"], b, k)
                bank_free(b, k, ax_kept, z_split, 2)
                aggregate(bank_agg, x2[:, k % 2], an_t[:, k // GROUP % 2, k % GROUP], KT, ax_done)

            def l2_product(b, k):
                made(pe, ax_kept, b, k)
                bank_free(b, k, y_ready["l2"], ax3_kept, -2)
                product(bank_l2, ax_t[:, k % 2], wl2, KT, l2_done)

            def l3_sources(b, k):
                made(pe, wh1_ready, b, k)
                bank_free(b, k, z_att_ready, adj_kept, 4)
                pe.transpose(bank_adj[:, 0:P], wh[:, k % 2, 0:1].to_broadcast([P, P]),
                             identity[:]).then_inc(src_done, 1)

            def l3_aggregate(b, k):
                made(pe, att_ready, b, k)
                bank_free(b, k, ax3_kept, y_ready["l2"], 1)
                aggregate(bank_l2, x3[:, k % 2], att_t[:, k % 2], KT, ax3_done)

            def l3_product(b, k):
                made(pe, ax3_kept, b, k)
                freed(pe, relu_h_ready, b, k, 1)
                product(bank_l3, ax3_t[:, k % 2], wl3, KT, l3_done)

            def step(b, k):
                stage(l2_aggregate, b, k, 6)
                stage_begun(stage, l0_project, b, k, 2)
                stage(l2_product, b, k, 6)
                stage(adjacency, b, k, 2)
                stage(conv2_product, b, k, 5)
                stage(l3_aggregate, b, k, 7)
                stage(conv1_aggregate, b, k, 3)
                stage(l0_aggregate, b, k, 2)
                stage(l3_product, b, k, 7)
                stage_once(constant_rows, b, k, 4)
                stage(conv1_product, b, k, 3)
                stage(l3_sources, b, k, 6)
                stage(conv2_aggregate, b, k, 4)
            l0_project(0, 0)
            first_degree_rows()
            run(pe, step)

        @block.scalar
        def _(act):
            def round_w0(c):
                act.wait_ge(w0_loaded[c], 16)
                act.activation(w0_hi[:, c], w0_raw[:, c], ACT.Copy).then_inc(w0_rounded, 1)

            def round_w1():
                act.wait_ge(w1_loaded, 16)
                act.activation(w1_hi[:], w1_raw[:], ACT.Copy).then_inc(w1_rounded, 1)

            def round_w2():
                act.wait_ge(w2_scaled, 1)
                act.activation(w2_hi[:], w2_gamma[:], ACT.Copy).then_inc(w2_rounded, 1)

            def edge_weights(b, k):
                i = k // GROUP % 2
                if not isinstance(b, int) or b + k >= 2 * GROUP:
                    act.wait_ge(adj_done, b + (k - GROUP))
                else:
                    act.wait_ge(consts_set, 3)
                loaded(act, at_loaded, b, k)
                act.activation(s_rhs[:, i, :, P:P + 1], at_in[:, i, :, 0:1],
                               ACT.Copy).then_inc(w_col_ready, GROUP)

            def keep_adj(b, k):
                made(act, adj_done, b, k)
                act.activation(adj_sb[:, k % 8], bank_adj[:, 0:P + 2],
                               ACT.Copy).then_inc(adj_kept, 1)

            def round_xt(b, k):
                if first(b, k):
                    act.wait_ge(x0_loaded, 16)
                else:
                    loaded(act, xt_loaded, b, k)
                freed(act, l0_projected, b, k)
                act.activation(xt_hi[:, k % 2], xt_in[:, k // GROUP % 2, k % GROUP],
                               ACT.Copy).then_inc(xt_rounded, 1)

            def keep_pb(b, k):
                made(act, l0_projected, b, k)
                freed(act, l0_done, b, k)
                act.activation(pb_sb[:, k % 2], bank_l0[:, F:2 * F], ACT.Copy).then_inc(pb_kept, 1)

            def round_z(b, k):
                made(act, sx_done, b, k)
                freed(act, conv1_done, b, k)
                act.activation(z_hi[:, k % 2], bank_agg[:, 0:KT * P], ACT.Copy).then_inc(z_rounded, 1)

            def relu_u(b, k):
                r = k % 2
                made(act, u_ready, b, k)
                freed(act, normed["l1a"], b, k)
                act.activation(h[:, r], u[:, r], ACT.Relu, accum_out=y_sum["l1a"][:, r:r + 1])\
                    .then_inc(h_relu, 1)

            def round_sh(b, k):
                made(act, sh_done, b, k)
                freed(act, conv2_done, b, k)
                act.activation(sh_hi[:, k % 2], bank_sh[:], ACT.Copy).then_inc(sh_rounded, 1)

            def base_beta(b, k):
                pair_made(act, dn_rowsum_ready, b, k)
                if first(b, k):
                    act.wait_ge(rows_kept, 1)
                freed(act, base_b_ready, b, k)
                act.activation(base_a[:, k % 2], w2_beta_row[:], ACT.Copy,
                               scale=dn_rowsum[:, k % 8:k % 8 + 1]).then_inc(base_a_ready, 1)

            def keep_ax(b, k):
                made(act, ax_done, b, k)
                freed(act, l2_done, b, k)
                act.activation(ax_t[:, k % 2], bank_agg[:, 0:KT * P], ACT.Copy).then_inc(ax_kept, 1)

            def exp_att(b, k):
                r = k % 2
                made(act, nm_att_ready, b, k)
                freed(act, att_ready, b, k)
                act.activation(p_att[:, r], em_att[:, r], ACT.Exp, bias=nm_att[:, r:r + 1],
                               accum_out=sum_att[:, r:r + 1]).then_inc(p_att_ready, 1)

            def keep_ax3(b, k):
                made(act, ax3_done, b, k)
                freed(act, l3_done, b, k)
                act.activation(ax3_t[:, k % 2], bank_l2[:, 0:KT * P], ACT.Copy).then_inc(ax3_kept, 1)

            def exp_elu(b, k):
                made(act, l3_done, b, k)
                freed(act, y_ready["l3"], b, k)
                act.activation(exp_h[:, k % 2], bank_l3[:, 0:F], ACT.Exp).then_inc(exp_ready, 1)

            def relu_elu(b, k):
                made(act, l3_done, b, k)
                freed(act, elu_x_ready, b, k)
                act.activation(relu_h[:, k % 2], bank_l3[:, 0:F], ACT.Relu).then_inc(relu_h_ready, 1)

            def root(n):
                return WIDTH[n] ** -0.5

            def means(b, k, n):
                r = k % 2
                made(act, y_ready[n], b, k)
                freed(act, normed[n], b, k)
                act.activation(mean_var[n][:, r, 0:1], y_sum[n][:, r:r + 1], ACT.Copy,
                               scale=(-1.0 if n == "l3" else 1.0) / WIDTH[n])
                act.activation(shift[n][:, r:r + 1], y_sum[n][:, r:r + 1], ACT.Copy,
                               scale=-root(n) / WIDTH[n]).then_inc(means_ready[n], 1)

            def variance(b, k, n):
                r = k % 2
                made(act, means_ready[n], b, k)
                act.activation(squares[n][:, r], Y[n][:, r], ACT.Square, scale=root(n),
                               bias=shift[n][:, r:r + 1],
                               accum_out=mean_var[n][:, r, 1:2]).then_inc(moments_ready[n], 1)

            def shift_l3(b, k):
                r = k % 2
                made(act, rstd_ready["l3"], b, k)
                act.activation(shift_std[:, r:r + 1], mean_var["l3"][:, r, 0:1], ACT.Copy,
                               scale=rstd["l3"][:, r:r + 1]).then_inc(shift_std_ready, 1)

            def norm_l3(b, k):
                r, i, j = k % 2, k // GROUP % 2, k % GROUP
                made(act, shift_std_ready, b, k)
                if j == 0:
                    act.wait_ge(stored[i], b * 2 + (k // UNROLL * 16 + 16))
                act.activation(out_st[:, i, j], y3[:, r], ACT.Identity, scale=rstd["l3"][:, r:r + 1],
                               bias=shift_std[:, r:r + 1]).then_inc(normed["l3"], 1)

            def step(b, k):
                stage(base_beta, b, k, 4)
                stage(variance, b, k, 2, "l0")
                stage(round_sh, b, k, 4)
                stage(keep_ax, b, k, 5)
                stage_once(round_w2, b, k, 3)
                stage(relu_u, b, k, 3)
                stage(exp_att, b, k, 6)
                stage(means, b, k, 7, "l3")
                stage(variance, b, k, 7, "l3")
                stage(keep_pb, b, k, 1)
                stage_once(round_w1, b, k, 1)
                stage(keep_adj, b, k, 1)
                stage(means, b, k, 3, "l1a")
                stage(variance, b, k, 3, "l1a")
                stage(keep_ax3, b, k, 6)
                stage(round_z, b, k, 2)
                stage_begun(stage, round_xt, b, k, 0)
                stage(means, b, k, 4, "l1b")
                stage(variance, b, k, 4, "l1b")
                stage(shift_l3, b, k, 7)
                stage(exp_elu, b, k, 6)
                stage_group(edge_weights, b, k, 0)
                stage(relu_elu, b, k, 6)
                stage(norm_l3, b, k, 7)
                stage(means, b, k, 1, "l0")
            round_xt(0, 0)
            for c in range(KT):
                round_w0(c)
            run(act, step)

        @block.vector
        def _(dve):
            def stats_of(b, k, n):
                r = k % 2
                made(dve, y_ready[n], b, k)
                freed(dve, moments_ready[n], b, k)
                dve.bn_stats(stats[n][:, r], Y[n][:, r]).then_inc(stats_ready[n], 1)

            def moments(b, k, n):
                made_for_plain(dve, stats_ready[n], b, k)
                dve.bn_aggr(mean_var[n][:, k % 2], stats[n][:, k % 2]).then_inc(moments_ready[n], 1)

            def norm_apply(n, dst, b, k):
                r = k % 2
                dve.tensor_scalar(dst, Y[n][:, r], mean_var[n][:, r, 0:1], rstd[n][:, r:r + 1],
                                  ALU.subtract, ALU.mult).then_inc(normed[n], 1)

            dve.memset(minus_half[:], -0.5).then_inc(consts_set, 1)
            for i in range(2):
                dve.memset(out_st[:, i, 0, 0:1], 0.0).then_inc(stored[i], 16)
            dve.memset(eps_col[:], EPS_LN).then_inc(consts_set, 1)
            dve.memset(s_rhs[:, :, :, P + 1:P + 2], 1.0).then_inc(consts_set, 1)

            def split_w0(c):
                dve.wait_ge(w0_rounded, c + 1)
                dve.tensor_tensor(w0_lo[:, c], w0_raw[:, c], w0_hi[:, c].bitcast(F32), ALU.subtract)\
                    .then_inc(w0_split, 1)

            def split_w1():
                dve.wait_ge(w1_rounded, 1)
                dve.tensor_tensor(w1_lo[:], w1_raw[:], w1_hi[:].bitcast(F32), ALU.subtract)\
                    .then_inc(w1_split, 1)

            def scale_w2():
                dve.wait_ge(late_loads, 16 * LATE)
                for c in range(HT):
                    ins = dve.tensor_scalar(w2_gamma[:, c], w2_raw[:, c], gamma_col[:, c:c + 1], None,
                                            ALU.mult)
                ins.then_inc(w2_scaled, 1)

            def split_w2():
                dve.wait_ge(w2_rounded, 1)
                dve.tensor_tensor(w2_lo[:], w2_gamma[:], w2_hi[:].bitcast(F32), ALU.subtract)\
                    .then_inc(w2_split, 1)

            def keep_rows():
                dve.wait_ge(rows_made, 1)
                dve.tensor_copy(w2_beta_row[:], bank_conv2[:, 0:F])
                dve.tensor_copy(wa_row[:, 0], bank_l2[:, 0:F])
                dve.tensor_copy(wa_row[:, 1], bank_l3[:, 0:F]).then_inc(rows_kept, 1)

            def degrees(b, k):
                i = k // GROUP % 2
                loaded(dve, a_loaded, b, k)
                dve.tensor_reduce(deg[:, i], a_in[:, i], AX.X, ALU.add).then_inc(deg_sum, GROUP)

            def degree_scales(b, k):
                i = k // GROUP % 2
                group_made(dve, deg_sum, b, k)
                dve.tensor_scalar(deg_max[:, i], deg[:, i], EPS_DEG, None, ALU.max)\
                    .then_inc(deg_clamped, GROUP)
                group_made(dve, deg_clamped, b, k)
                if not isinstance(b, int) or b + k >= 3 * GROUP:
                    dve.wait_ge(deg_stored, b * 4 + (k * 4 - 32))
                dve.reciprocal(deg_inv[:, i], deg_max[:, i]).then_inc(deg_inverted, GROUP)

            def degree_ratio(b, k):
                i = k // GROUP % 2
                dve.reciprocal(deg_raw_inv[:, i], deg[:, i]).then_inc(deg_raw_inverted, GROUP)
                group_made(dve, deg_raw_inverted, b, k)
                dve.tensor_tensor(deg_ratio[:, i], deg_max[:, i], deg_raw_inv[:, i], ALU.mult)\
                    .then_inc(ratio_ready, GROUP)

            def incidence(b, k):
                i = k // GROUP % 2
                loaded(dve, at_loaded, b, k)
                if not isinstance(b, int) or b + k >= 2 * GROUP:
                    dve.wait_ge(adj_done, b + (k - GROUP))
                dve.tensor_scalar(h_t[:, i], at_in[:, i], 0.0, None, ALU.not_equal)\
                    .then_inc(h_ready, GROUP)

            def count_edges(b, k):
                i = k // GROUP % 2
                group_made(dve, h_ready, b, k)
                dve.tensor_reduce(edge_n[:, i], h_t[:, i], AX.X, ALU.add)\
                    .then_inc(edges_counted, GROUP)

            def edge_scale(b, k):
                i = k // GROUP % 2
                group_made(dve, edges_counted, b, k)
                dve.tensor_scalar(edge_n1[:, i], edge_n[:, i], 1.0, None, ALU.max)\
                    .then_inc(edges_clamped, GROUP)
                group_made(dve, edges_clamped, b, k)
                dve.reciprocal(edge_inv[:, i], edge_n1[:, i]).then_inc(edges_inverted, GROUP)

            def masks(b, k):
                i = k // GROUP % 2
                dve.tensor_scalar(mask[:, i], at_in[:, i], 0.5, None, ALU.is_gt)\
                    .then_inc(mask_ready, GROUP)
                dve.tensor_scalar(penalty[:, i], at_in[:, i], 0.5, NEG_INF, ALU.is_le, ALU.mult)\
                    .then_inc(penalty_ready, GROUP)

            def node_scale(b, k):
                s = k % 8 - 1
                raw = adj_sb[:, s:s + 2, P]
                made(dve, adj_kept, b, k)
                dve.tensor_scalar(dn_max[:, s:s + 2], raw, TINY, None, ALU.max).then_inc(dn_clamped, 2)
                pair_made(dve, dn_clamped, b, k)
                dve.reciprocal(dn_rec[:, s:s + 2], dn_max[:, s:s + 2]).then_inc(dn_inverted, 2)
                pair_made(dve, dn_inverted, b, k)
                dve.scalar_tensor_tensor(out=dn[:, s:s + 2], in0=raw, scalar=0.0, in1=dn_rec[:, s:s + 2],
                                         op0=ALU.is_gt, op1=ALU.mult).then_inc(dn_ready, 2)
                pair_made(dve, dn_ready, b, k)
                dve.tensor_tensor(dn_rowsum[:, s:s + 2], dn[:, s:s + 2], adj_sb[:, s:s + 2, P + 1],
                                  ALU.mult).then_inc(dn_rowsum_ready, 2)

            def l0_residual(b, k):
                r = k % 2
                made(dve, l0_done, b, k)
                loaded(dve, x_loaded, b, k)
                freed(dve, normed["l0"], b, k)
                dve.scalar_tensor_tensor(out=y0[:, r], in0=bank_l0[:, 0:F], scalar=0.0,
                                         in1=x_in[:, k // GROUP % 2, k % GROUP],
                                         op0=ALU.max, op1=ALU.add,
                                         accum_out=y_sum["l0"][:, r:r + 1])\
                    .then_inc(y_ready["l0"], 1)

            def l0_norm(b, k):
                made(dve, rstd_ready["l0"], b, k)
                freed(dve, sx_done, b, k)
                freed(dve, base_c_ready, b, k)
                norm_apply("l0", x1[:, k % 2], b, k)

            def split_z(b, k):
                r = k % 2
                made(dve, z_rounded, b, k)
                freed(dve, conv1_done, b, k)
                dve.tensor_tensor(z_lo[:, r], bank_agg[:, 0:KT * P], z_hi[:, r].bitcast(F32),
                                  ALU.subtract).then_inc(z_split, 1)

            def conv1_bias(b, k):
                r, s = k % 2, k % 8
                made(dve, conv1_done, b, k)
                pair_made(dve, dn_ready, b, k)
                freed(dve, h_relu, b, k)
                if first(b, k):
                    dve.wait_ge(late_loads, 16 * LATE)
                dve.scalar_tensor_tensor(out=u[:, r], in0=bank_conv1[:], scalar=dn[:, s:s + 1],
                                         in1=b1_row[:], op0=ALU.mult, op1=ALU.add)\
                    .then_inc(u_ready, 1)

            def l1a_norm(b, k):
                made(dve, rstd_ready["l1a"], b, k)
                freed(dve, sh_done, b, k)
                norm_apply("l1a", hn[:, k % 2], b, k)

            def split_sh(b, k):
                r = k % 2
                made(dve, sh_rounded, b, k)
                freed(dve, conv2_done, b, k)
                dve.tensor_tensor(sh_lo[:, r], bank_sh[:], sh_hi[:, r].bitcast(F32),
                                  ALU.subtract).then_inc(sh_split, 1)

            def l1_residual(b, k):
                r, s = k % 2, k % 8
                made(dve, conv2_done, b, k)
                made(dve, base_ready, b, k)
                freed(dve, normed["l1b"], b, k)
                dve.scalar_tensor_tensor(out=y1[:, r], in0=bank_conv2[:, 0:F], scalar=dn[:, s:s + 1],
                                         in1=base[:, r], op0=ALU.mult, op1=ALU.add,
                                         accum_out=y_sum["l1b"][:, r:r + 1])\
                    .then_inc(y_ready["l1b"], 1)

            def l1b_norm(b, k):
                made(dve, rstd_ready["l1b"], b, k)
                freed(dve, ax_done, b, k)
                freed(dve, x2_b_ready, b, k)
                norm_apply("l1b", x2[:, k % 2], b, k)

            def l2_residual(b, k):
                r = k % 2
                made(dve, l2_done, b, k)
                made(dve, x2_b_ready, b, k)
                freed(dve, normed["l2"], b, k)
                dve.scalar_tensor_tensor(out=y2[:, r], in0=bank_l2[:, 0:F],
                                         scalar=deg_ratio_ring[:, k % 8:k % 8 + 1],
                                         in1=x2_b[:, r], op0=ALU.mult, op1=ALU.add)\
                    .then_inc(y_ready["l2"], 1)

            deg_ratio_ring = deg_ratio[:].rearrange("p i j -> p (i j)")

            def l2_norm(b, k):
                made(dve, rstd_ready["l2"], b, k)
                freed(dve, ax3_done, b, k)
                freed(dve, elu_x_ready, b, k)
                norm_apply("l2", x3[:, k % 2], b, k)

            def node_scores(b, k, a, ready):
                r = k % 2
                made(dve, normed["l2"], b, k)
                freed(dve, (src_done, z_att_ready)[a], b, k)
                dve.tensor_tensor_reduce(junk[:, r, a], x3[:, r], wa_row[:, a], 1.0, 0.0,
                                         ALU.mult, ALU.add, wh[:, r, a:a + 1]).then_inc(ready, 1)

            def src_weight(b, k):
                node_scores(b, k, 0, wh1_ready)

            def dst_weight(b, k):
                node_scores(b, k, 1, wh2_ready)

            def scores(b, k):
                r, i, j = k % 2, k // GROUP % 2, k % GROUP
                made(dve, src_done, b, k)
                made(dve, wh2_ready, b, k)
                group_made(dve, mask_ready, b, k)
                freed(dve, p_att_ready, b, k)
                dve.scalar_tensor_tensor(out=z_att[:, r], in0=bank_adj[:, 0:P], scalar=wh[:, r, 1:2],
                                         in1=mask[:, i, j], op0=ALU.add, op1=ALU.mult)\
                    .then_inc(z_att_ready, 1)

            def leaky(b, k):
                r = k % 2
                made(dve, z_att_ready, b, k)
                dve.scalar_tensor_tensor(out=e_att[:, r], in0=z_att[:, r], scalar=ALPHA,
                                         in1=z_att[:, r], op0=ALU.mult, op1=ALU.max)\
                    .then_inc(e_att_ready, 1)

            def masked(b, k):
                r, i, j = k % 2, k // GROUP % 2, k % GROUP
                made_for_plain(dve, e_att_ready, b, k)
                dve.tensor_tensor_reduce(em_att[:, r], e_att[:, r], penalty[:, i, j], 1.0, LOWEST,
                                         ALU.add, ALU.max, m_att[:, r:r + 1]).then_inc(em_att_ready, 1)

            def neg_max(b, k):
                r = k % 2
                made(dve, em_att_ready, b, k)
                dve.tensor_scalar(nm_att[:, r:r + 1], m_att[:, r:r + 1], -1.0, None, ALU.mult)\
                    .then_inc(nm_att_ready, 1)

            def att_inv(b, k):
                r = k % 2
                made(dve, p_att_ready, b, k)
                dve.reciprocal(inv_att[:, r:r + 1], sum_att[:, r:r + 1]).then_inc(inv_att_ready, 1)

            def attention(b, k):
                r = k % 2
                made(dve, inv_att_ready, b, k)
                freed(dve, ax3_done, b, k)
                dve.tensor_scalar(att_t[:, r], p_att[:, r], inv_att[:, r:r + 1], None, ALU.mult)\
                    .then_inc(att_ready, 1)

            def l3_residual(b, k):
                r = k % 2
                made(dve, elu_x_ready, b, k)
                made(dve, exp_ready, b, k)
                freed(dve, normed["l3"], b, k)
                dve.scalar_tensor_tensor(out=y3[:, r], in0=exp_h[:, r], scalar=1.0, in1=elu_x[:, r],
                                         op0=ALU.min, op1=ALU.add,
                                         accum_out=y_sum["l3"][:, r:r + 1])\
                    .then_inc(y_ready["l3"], 1)

            def step(b, k):
                stage_begun(stage_group, incidence, b, k, 0)
                stage_begun(stage_group, edge_scale, b, k, 1)
                stage_group(degree_ratio, b, k, 3)
                stage(neg_max, b, k, 7)
                stage(split_sh, b, k, 5)
                stage(l0_norm, b, k, 3)
                stage(att_inv, b, k, 7)
                stage(l2_residual, b, k, 6)
                stage(attention, b, k, 7)
                stage(stats_of, b, k, 6, "l2")
                stage_begun(stage_group, degree_scales, b, k, 1)
                stage_begun(stage_group, count_edges, b, k, 0)
                stage_once(split_w2, b, k, 4)
                stage(moments, b, k, 6, "l2")
                stage_group(masks, b, k, 2)
                stage_pair(node_scale, b, k, 2)
                stage(l1_residual, b, k, 5)
                stage_begun(stage_group, degrees, b, k, 0)
                stage(split_z, b, k, 3)
                stage(l2_norm, b, k, 6)
                stage(l1a_norm, b, k, 4)
                stage(src_weight, b, k, 6)
                stage(l0_residual, b, k, 2)
                stage(dst_weight, b, k, 6)
                stage(l1b_norm, b, k, 5)
                stage_once(split_w1, b, k, 2)
                stage_once(scale_w2, b, k, 3)
                stage(scores, b, k, 6)
                stage_once(keep_rows, b, k, 4)
                stage(conv1_bias, b, k, 3)
                stage(leaky, b, k, 6)
                stage(l3_residual, b, k, 7)
                stage(masked, b, k, 6)
            for c in range(KT):
                split_w0(c)
            for f in (degrees, degree_scales, incidence, count_edges, edge_scale):
                f(0, 0)
            dve.wait_ge(degree_rows_made, 1)
            dve.tensor_tensor(an_t[:, 0], at_in[:, 0], bank_l3[:].rearrange("p (g n) -> p g n", g=GROUP),
                              ALU.mult).then_inc(an_ready, GROUP)
            run(dve, step)

        @block.gpsimd
        def _(pool):
            def add_eps(b, k, n):
                r = k % 2
                made(pool, moments_ready[n], b, k)
                freed(pool, normed[n], b, k)
                pool.tensor_tensor(var_eps[n][:, r:r + 1], mean_var[n][:, r, 1:2], eps_col[:],
                                   ALU.add).then_inc(var_eps_ready[n], 1)

            def power(b, k, n):
                r = k % 2
                made(pool, var_eps_ready[n], b, k)
                pool.tensor_tensor(rstd[n][:, r:r + 1], var_eps[n][:, r:r + 1], minus_half[:],
                                   ALU.pow).then_inc(rstd_ready[n], 1)

            def scale_group(b, k):
                i = k // GROUP % 2
                pool.wait_ge(deg_row_loaded[i], b * 2 + (k // UNROLL * 16 + i * 16))
                loaded(pool, at_loaded, b, k)
                if not isinstance(b, int) or b + k >= 2 * GROUP:
                    pool.wait_ge(ax_done, b + (k - GROUP))
                pool.tensor_tensor(an_t[:, i], at_in[:, i], deg_row[:, i].rearrange("p n g -> p g n"),
                                   ALU.mult).then_inc(an_ready, GROUP)

            def scale_edges(b, k):
                i = k // GROUP % 2
                group_made(pool, edges_inverted, b, k)
                pool.tensor_tensor(s_rhs[:, i, :, 0:P], h_t[:, i],
                                   edge_inv[:, i].unsqueeze(2).to_broadcast([P, GROUP, P]),
                                   ALU.mult).then_inc(s_rhs_ready, GROUP)

            def split_xt(b, k):
                r = k % 2
                made(pool, xt_rounded, b, k)
                freed(pool, l0_projected, b, k)
                pool.tensor_tensor(xt_lo[:, r], xt_in[:, k // GROUP % 2, k % GROUP],
                                   xt_hi[:, r].bitcast(F32), ALU.subtract).then_inc(xt_split, 1)

            def base_bias(b, k):
                r = k % 2
                made(pool, base_a_ready, b, k)
                freed(pool, base_ready, b, k)
                if first(b, k):
                    pool.wait_ge(late_loads, 16 * LATE)
                pool.tensor_tensor(base_b[:, r], base_a[:, r], b2_row[:], ALU.add)\
                    .then_inc(base_b_ready, 1)

            def base_double(b, k):
                r = k % 2
                made_for_plain(pool, normed["l0"], b, k)
                freed(pool, base_ready, b, k)
                pool.tensor_scalar(base_c[:, r], x1[:, r], 2.0, 0.0, ALU.mult, ALU.add)\
                    .then_inc(base_c_ready, 1)

            def base_sum(b, k):
                r = k % 2
                made(pool, base_b_ready, b, k)
                made(pool, base_c_ready, b, k)
                freed(pool, y_ready["l1b"], b, k)
                pool.tensor_tensor(base[:, r], base_b[:, r], base_c[:, r], ALU.add)\
                    .then_inc(base_ready, 1)

            def elu_sum(b, k):
                r = k % 2
                made(pool, relu_h_ready, b, k)
                made(pool, normed["l2"], b, k)
                freed(pool, y_ready["l3"], b, k)
                pool.tensor_tensor(elu_x[:, r], relu_h[:, r], x3[:, r], ALU.add)\
                    .then_inc(elu_x_ready, 1)

            def l2_bias(b, k):
                made(pool, normed["l1b"], b, k)
                freed(pool, y_ready["l2"], b, k)
                pool.tensor_tensor(x2_b[:, k % 2], x2[:, k % 2], bl2_row[:], ALU.add)\
                    .then_inc(x2_b_ready, 1)

            def step(b, k):
                if first(b, k):
                    pool.wait_ge(consts_set, 3)
                stage(add_eps, b, k, 6, "l2")
                stage(add_eps, b, k, 4, "l1a")
                stage(power, b, k, 6, "l2")
                stage(power, b, k, 4, "l1a")
                stage_begun(stage, split_xt, b, k, 1)
                stage(add_eps, b, k, 5, "l1b")
                stage(power, b, k, 5, "l1b")
                stage(elu_sum, b, k, 7)
                stage(l2_bias, b, k, 5)
                stage(base_bias, b, k, 4)
                stage(add_eps, b, k, 2, "l0")
                stage(power, b, k, 2, "l0")
                stage_begun(stage_group, scale_group, b, k, 1)
                stage(base_sum, b, k, 4)
                stage_group(scale_edges, b, k, 0)
                stage(add_eps, b, k, 7, "l3")
                stage(base_double, b, k, 2)
                stage(power, b, k, 7, "l3")
            split_xt(0, 0)
            run(pool, step)


def kernel(x, adj, L0_gnn_W, L1_gnn_W1, L1_gnn_b1, L1_gnn_gamma, L1_gnn_beta, L1_gnn_W2, L1_gnn_b2,
           L2_gnn_W, L2_gnn_b, L3_gnn_W, L3_gnn_a):
    import numpy as np
    import concourse.bacc as bacc
    from concourse.bass_utils import run_bass_kernel_spmd

    x, adj = np.asarray(x), np.asarray(adj)
    n, p, f = x.shape
    groups, kt = n // GROUP, f // p

    def rows(w):
        w = np.asarray(w)
        return w.reshape(w.shape[0] // p, p, w.shape[1]).transpose(1, 0, 2)

    def cols(v):
        return np.asarray(v).reshape(-1, p).T

    w0, w3 = np.asarray(L0_gnn_W), np.asarray(L3_gnn_W)
    arrays = {
        "x_nodes": x.reshape(groups, GROUP, p, f).transpose(0, 2, 1, 3),
        "x_feats": x.reshape(groups, GROUP, p, kt, p).transpose(0, 4, 1, 3, 2),
        "adj_rows": adj.reshape(groups, GROUP, p, p).transpose(0, 2, 1, 3),
        "adj_cols": adj.reshape(groups, GROUP, p, p).transpose(0, 3, 1, 2),
        "ident": np.eye(p, dtype=x.dtype),
        "w0_t": rows(np.concatenate([w0[:, :f].T, w0[:, f:].T], axis=1)),
        "w1_t": rows(np.asarray(L1_gnn_W1).T),
        "b1": np.asarray(L1_gnn_b1),
        "gamma": cols(L1_gnn_gamma),
        "beta": cols(L1_gnn_beta),
        "w2_t": rows(np.asarray(L1_gnn_W2).T),
        "b2": np.asarray(L1_gnn_b2),
        "w_l2": rows(L2_gnn_W),
        "b_l2": np.asarray(L2_gnn_b),
        "w_l3": rows(w3),
        "w_l3_t": rows(w3.T),
        "attn": cols(L3_gnn_a),
    }
    nc = bacc.Bacc("TRN2", target_bir_lowering=False, num_devices=1)
    ins, args = {}, []
    for name, a in arrays.items():
        a = np.ascontiguousarray(a)
        ins[f"in_{name}"] = a
        args.append(nc.dram_tensor(f"in_{name}", a.shape, mybir.dt.from_np(a.dtype),
                                   kind="ExternalInput").ap())
    out = nc.dram_tensor("out_x", (groups, p, GROUP, f), F32, kind="ExternalOutput").ap()
    degrees_dram = nc.dram_tensor("degrees_dram", (groups, p, GROUP), F32, kind="Internal").ap()
    build(nc, *args, degrees_dram, out)
    r = run_bass_kernel_spmd(nc, [ins], core_ids=[0])
    got = r.results[0]["out_x"]
    return np.ascontiguousarray(got.transpose(0, 2, 1, 3)).reshape(n, p, f)
```
